# Optimizing a Trainium2 kernel written in Bass

```python
import numpy as np
import jax
import jax.numpy as jnp

def _softmax(x, axis=-1):
    return jax.nn.softmax(x, axis=axis)

def _gelu(x):
    return jax.nn.gelu(x, approximate=True)

def _silu(x):
    return jax.nn.silu(x)

def _sigmoid(x):
    return jax.nn.sigmoid(x)

def _layernorm(x, axis=-1, eps=1e-05):
    m = jnp.mean(x, axis=axis, keepdims=True)
    v = jnp.var(x, axis=axis, keepdims=True)
    return (x - m) / jnp.sqrt(v + eps)

def _scatter_add(tgt, idx, src, axis=0):
    return tgt.at[idx].add(src)

def _segment_sum(src, seg, n):
    return jax.ops.segment_sum(src, seg, n)
kernel_name = 'mk_adj_resnorm_d1_adj_r2_fed3f9'

def setup_inputs(seed: int=0):
    np.random.seed(seed)
    _w = jnp.asarray

    def _rec_inputs():
        import jax
        import jax.numpy as jnp
        _gk = jax.random.key(seed)
        x = -0.001547 + 1.001 * jax.random.normal(jax.random.fold_in(_gk, 1), (8192, 64), jnp.float32)
        _w = (1.0 + jnp.arange(8192, dtype=jnp.float32)) ** (-0.5)
        _w = _w / _w.mean()
        _pij = jnp.clip(0.000488281 * _w[:, None] * _w[None, :], 0.0, 1.0)
        _a = jax.random.uniform(jax.random.fold_in(_gk, 2), (8192, 8192)) < _pij
        _a = jnp.logical_or(_a, jnp.eye(8192, dtype=bool))
        _af = _a.astype(jnp.float32)
        adj = _af
        return (x, adj)
    x, adj = _rec_inputs()

    def _L0_gnn_setup():
        import jax, jax.numpy as jnp
        import numpy as np
        N = 2048
        F = 64
        H = 8
        D = 8
        key = jax.random.key(seed)
        k1, k2, k3, k4, k5, k6 = jax.random.split(key, 6)
        X = jax.random.normal(k1, (N, F), dtype=jnp.float32)
        A = (jax.random.uniform(k2, (N, N)) < 0.01).astype(jnp.float32)
        A = jnp.maximum(A, jnp.eye(N, dtype=jnp.float32))
        lim_w = np.sqrt(6.0 / (F + H * D)).astype(np.float32)
        W = jax.random.uniform(k3, (F, H * D), minval=-lim_w, maxval=lim_w, dtype=jnp.float32)
        lim_a = np.sqrt(6.0 / (1 + H * D)).astype(np.float32)
        att_self = jax.random.uniform(k4, (H, D), minval=-lim_a, maxval=lim_a, dtype=jnp.float32)
        att_neigh = jax.random.uniform(k5, (H, D), minval=-lim_a, maxval=lim_a, dtype=jnp.float32)
        bias = jnp.zeros((H, D), dtype=jnp.float32)
        return {'X': X, 'A': A, 'W': W, 'att_self': att_self, 'att_neigh': att_neigh, 'bias': bias}
    _L0_gnn_all = _L0_gnn_setup()
    _L0_gnn_in = {k: v for k, v in _L0_gnn_all.items() if k in ('W', 'att_self', 'att_neigh', 'bias')}
    del _L0_gnn_all
    return {'x': x, 'adj': adj, 'L0_gnn_W': _L0_gnn_in['W'], 'L0_gnn_att_self': _L0_gnn_in['att_self'], 'L0_gnn_att_neigh': _L0_gnn_in['att_neigh'], 'L0_gnn_bias': _L0_gnn_in['bias']}

def reference(x, adj, L0_gnn_W, L0_gnn_att_self, L0_gnn_att_neigh, L0_gnn_bias):
    import jax
    import jax.numpy as jnp

    def _L0_gnn_ref(X, A, W, att_self, att_neigh, bias):
        import jax, jax.numpy as jnp
        import numpy as np
        N = 2048
        F = 64
        H = 8
        D = 8
        feats = (X @ W).reshape(-1, H, D)
        a_self = jnp.einsum('nhd,hd->nh', feats, att_self)
        a_neigh = jnp.einsum('nhd,hd->nh', feats, att_neigh)
        scores = a_self.T[:, :, None] + a_neigh.T[:, None, :]
        scores = jax.nn.leaky_relu(scores, negative_slope=0.2)
        scores = scores + (-10000000000.0 * (1.0 - A))[None, :, :]
        attn = jax.nn.softmax(scores, axis=-1)
        out = jnp.einsum('hij,jhd->ihd', attn, feats)
        out = out + bias[None, :, :]
        out = out.reshape(-1, H * D)
        return jax.nn.relu(out)
    x = _layernorm(x + _L0_gnn_ref(x, adj, L0_gnn_W, L0_gnn_att_self, L0_gnn_att_neigh, L0_gnn_bias), axis=-1)
    return x

_drawn_inputs = setup_inputs


def setup_inputs(seed=0):
    import zlib

    import numpy as np

    out = dict(_drawn_inputs(seed))
    spreads = {'L0_gnn_bias': (0.0, 0.1)}
    factors = {}
    for name, (base, spread) in spreads.items():
        noise = np.random.default_rng([zlib.crc32(name.encode()), seed]).standard_normal(out[name].shape)
        drawn = base * np.exp(spread * noise) if base else spread * noise
        out[name] = jnp.asarray(drawn.astype(out[name].dtype))
    for name, factor in factors.items():
        out[name] = (out[name] * factor).astype(out[name].dtype)
    return out
```

```python
import concourse.bass as bass
from concourse import mybir
from contextlib import ExitStack


def gat_resnorm(nc, x, adj, w, att_self, att_neigh, bias, out):
    fp32, bf16 = mybir.dt.float32, mybir.dt.bfloat16
    i32, u32 = mybir.dt.int32, mybir.dt.uint32
    ALU, ACT, AX = mybir.AluOpType, mybir.ActivationFunctionType, mybir.AxisListType

    N, F = x.shape
    H, D = att_self.shape
    P = 128
    NB = N // P
    BITS = 16
    GC = N // BITS
    HALF = N // 2
    TC = 2 * H + F
    GB = 4
    NG = NB // GB
    SLOPE = 0.2
    EPS = 1e-5
    FAR = -1e30
    R = 16
    J = N // P
    EARLY = [56] + [32] * 7
    SLOTS = 16
    S_MAX = max(EARLY)
    NE = len(EARLY)

    def slots(b):
        return EARLY[b] if b < NE else SLOTS

    ctx = ExitStack()
    with ctx:
        def sb(name, shape, dt):
            return ctx.enter_context(nc.sbuf_tensor(name, shape, dt))

        def pb(name, shape, dt):
            return ctx.enter_context(nc.psum_tensor(name, shape, dt))

        def sem(name):
            return ctx.enter_context(nc.semaphore(name))

        table = nc.dram_tensor("node_table", [N + 1, TC], fp32)

        adj_sb = sb("adj_sb", [P, 4, HALF], fp32)
        x_sb = sb("x_sb", [P, NB, F], fp32)
        own = sb("own", [P, NB, H], fp32)
        w_sb = sb("w_sb", [F, F], fp32)
        an_sb = sb("an_sb", [F, F], fp32)
        as_sb = sb("as_sb", [F, F], fp32)
        wtmp = sb("wtmp", [F, F], fp32)
        wa = sb("wa", [F, TC], fp32)
        bias_sb = sb("bias_sb", [P, F], fp32)
        ident = sb("ident", [P, P], fp32)
        weights = sb("weights", [P, BITS, P], bf16)
        mean_col = sb("mean_col", [P, 1], fp32)
        xsum = sb("xsum", [P, F], fp32)
        xmean = sb("xmean", [F, 1], fp32)
        dummy = sb("mean_row", [1, TC], fp32)
        one_i = sb("one_i", [P, BITS], i32)
        bit_i = sb("bit_i", [P, BITS], i32)
        pow_i = sb("pow_i", [P, BITS], i32)
        pow_f = sb("pow_f", [P, BITS], fp32)
        off_i = sb("off_i", [P, BITS], i32)
        off_f = sb("off_f", [P, BITS], fp32)
        work = sb("work", [P, GC], fp32)
        val = sb("val", [P, S_MAX], fp32)
        col = sb("col", [P, S_MAX], u32)
        val_i = sb("val_i", [P, S_MAX], i32)
        hit = sb("hit", [P, S_MAX, BITS], i32)
        keys = sb("keys", [P, S_MAX, BITS], fp32)
        key = sb("key", [P, S_MAX], fp32)
        idx = [sb(f"idx{i}", [P, S_MAX], u32) for i in range(2)]
        over = sb("over", [P, NB], fp32)
        near = [sb(f"near{i}", [P, S_MAX if i == 0 else max(EARLY[1:]), TC], fp32) for i in range(2)]
        z = sb("z", [P, S_MAX, H], fp32)
        lz = sb("lz", [P, S_MAX, H], fp32)
        top = sb("top", [P, H], fp32)
        prob = sb("prob", [P, S_MAX, H], fp32)
        den = sb("den", [P, H], fp32)
        rden = sb("rden", [P, H], fp32)
        num = sb("num", [P, F], fp32)
        att = sb("att", [P, F], fp32)
        y = sb("y", [P, F], fp32)
        bn6 = sb("bn6", [P, 6], fp32)
        mv = sb("mv", [P, 2], fp32)
        stats = sb("stats", [P, NB, 2], fp32)
        rstd = sb("rstd", [P, NB], fp32)
        std = sb("std", [P, NB], fp32)

        nodes = sb("nodes", [P, J, TC], fp32)
        score = sb("score", [P, J, R * H], fp32)
        spare = score[:, :, :].rearrange("p j k -> p (j k)")
        n_in, n_xt = 2 * GB * F, 2 * GB * P
        x_in = spare[:, 0:n_in].rearrange("p (i j f) -> p i j f", i=2, f=F)
        xt_sb = spare[0:F, n_in:n_in + n_xt].rearrange("p (i c) -> p i c", i=2)
        feat_sb = spare[:, n_in + n_xt:n_in + n_xt + 2 * GB * TC].rearrange("p (i j c) -> p i j c", i=2, c=TC)
        arow = sb("arow", [P, R, J], fp32)
        own_r = sb("own_r", [P, R, H], fp32)
        x_r = sb("x_r", [R, F], fp32)
        dmax = sb("dmax", [P, R * H], fp32)
        dcol = sb("dcol", [P, 1], fp32)
        dtile = sb("dtile", [P, R * H], fp32)
        drden = sb("drden", [P, 1], fp32)
        dnum = sb("dnum", [P, F], fp32)
        datt = sb("datt", [R, F], fp32)
        dy = sb("dy", [R, F], fp32)
        dbn6 = sb("dbn6", [R, 6], fp32)
        dmv = sb("dmv", [R, 2], fp32)
        dvar = sb("dvar", [R, 1], fp32)
        dstd = sb("dstd", [R, 1], fp32)
        drstd = sb("drstd", [R, 1], fp32)
        head8 = sb("head8", [P, H], fp32)
        head_mask = sb("head_mask", [P, F], fp32)
        row_sel = sb("row_sel", [P, R], fp32)
        group_sel = sb("group_sel", [P, P // R], fp32)
        NGR = N // R
        gflag_f = sb("gflag_f", [1, NB, P // R], fp32)
        gzero = work[0:1, 0:NGR]
        gcount = keys[0:1, 0:NGR // BITS, :].rearrange("o s k -> o (s k)")
        gflag = sb("gflag", [1, NGR], i32)
        gturn = sb("gturn", [1, NGR], i32)
        bflag = sb("bflag", [1, NB], i32)
        bflag_f = sb("bflag_f", [1, NB], fp32)

        codes = [pb(f"codes{i}", [P, GC], fp32) for i in range(2)]
        xt_ps = [pb(f"xt_ps{i}", [P, GB * P], fp32) for i in range(2)]
        ft_ps = [pb(f"ft_ps{i}", [P, GB * TC], fp32) for i in range(2)]
        mean_ps = pb("mean_ps", [P, P], fp32)
        flag_ps = pb("flag_ps", [1, NB * (P // R)], fp32)

        adj_loaded = [sem(f"adj_loaded{i}") for i in range(4)]
        params_loaded = sem("params_loaded")
        x_loaded = sem("x_loaded")
        xin_loaded = [sem(f"xin_loaded{i}") for i in range(2)]
        ident_ready = sem("ident_ready")
        iotas_ready = sem("iotas_ready")
        dve_done = sem("dve_done")
        consts_ready = sem("consts_ready")
        wa_ready = sem("wa_ready")
        x_transposed = sem("x_transposed")
        xt_copied = sem("xt_copied")
        feats_ready = sem("feats_ready")
        feats_copied = sem("feats_copied")
        table_written = [sem(f"table_written{i}") for i in range(2)]
        xsum_ready = sem("xsum_ready")
        xmean_made = sem("xmean_made")
        xmean_copied = sem("xmean_copied")
        dummy_made = sem("dummy_made")
        dummy_ready = sem("dummy_ready")
        dummy_written = sem("dummy_written")
        halves_packed = sem("halves_packed")
        codes_read = sem("codes_read")
        idx_ready = sem("idx_ready")
        gathered = [sem(f"gathered{i}") for i in range(2)]
        near_used = sem("near_used")
        scores_ready = sem("scores_ready")
        probs_ready = sem("probs_ready")
        stats_ready = sem("stats_ready")
        std_ready = sem("std_ready")
        out_ready = sem("out_ready")
        stored = sem("stored")
        nodes_loaded = sem("nodes_loaded")
        d_loaded = sem("d_loaded")
        d_max = sem("d_max")
        d_max_t = sem("d_max_t")
        d_max_col = sem("d_max_col")
        d_max_row = sem("d_max_row")
        d_scores = sem("d_scores")
        d_probs = sem("d_probs")
        d_sums = sem("d_sums")
        d_scaled = sem("d_scaled")
        d_rows = sem("d_rows")
        d_var = sem("d_var")
        d_std = sem("d_std")
        d_out = sem("d_out")
        d_stored = sem("d_stored")
        over_ready = sem("over_ready")
        groups_summed = sem("groups_summed")
        flags_ready = sem("flags_ready")
        waits_passed = sem("waits_passed")

        adj_v = adj.rearrange("(b p) (h c) -> b p h c", p=P, h=2)
        x_v = x.rearrange("(b p) f -> p b f", p=P)
        out_v = out.rearrange("(b p) f -> p b f", p=P)
        table_r = table[1:N + 1, :]
        table_v = table[1:N + 1, :].rearrange("(b p) c -> p b c", p=P)
        adj_bf = [adj_sb[:, q, :].bitcast(bf16).rearrange("p (c two) -> p c two", two=2) for q in range(4)]
        STORES = 4
        CH = NB // STORES

        def wait_apart(eng, signal, value):
            eng.wait_ge(signal, value)
            eng.sem_inc(waits_passed, 1)

        def flagged_groups(eng, body):
            eng.wait_ge(flags_ready, 1)
            with eng.Fori(0, NB) as b:
                any_group = eng.value_load(bflag[0:1, bass.ds(b, 1)], min_val=0, max_val=1)
                with eng.If(any_group > 0):
                    with eng.Fori(0, P // R) as q:
                        g = b * (P // R) + q
                        this_group = eng.value_load(gflag[0:1, bass.ds(g, 1)], min_val=0, max_val=1)
                        with eng.If(this_group > 0):
                            turn = eng.value_load(gturn[0:1, bass.ds(g, 1)], min_val=1, max_val=NGR)
                            body(g, turn)

        block = ctx.enter_context(nc.Block())

        @block.sync
        def _(sp):
            def load(b, par, first):
                for h in range(2):
                    if not first:
                        sp.wait_ge(halves_packed, 2 * b - 3 + h)
                    sp.dma_start(adj_sb[:, 2 * par + h, :], adj_v[b, :, h, :]).then_inc(adj_loaded[2 * par + h], 16)

            load(0, 0, True)
            load(1, 1, True)
            with sp.Fori(1, NB // 2) as t:
                load(2 * t, 0, False)
                load(2 * t + 1, 1, False)
            for c in range(STORES):
                sp.wait_ge(out_ready, c + 1)
                sp.dma_start(out_v[:, c * CH:(c + 1) * CH, :], x_sb[:, c * CH:(c + 1) * CH, :]).then_inc(stored, 16)
            sp.wait_ge(stored, 16 * STORES)

        @block.gpsimd
        def _(pool):
            pool.memset(ident[:, :], 0.0).then_inc(ident_ready, 1)
            pool.wait_ge(ident_ready, 1)
            pool.affine_select(out=ident[:, :], in_=ident[:, :], compare_op=ALU.not_equal, fill=1.0,
                               base=0, pattern=[[-1, P]], channel_multiplier=1).then_inc(ident_ready, 1)
            pool.iota(bit_i[:, :], [[1, BITS]], base=0, channel_multiplier=0).then_inc(iotas_ready, 1)
            pool.iota(off_i[:, :], [[GC, BITS]], base=1, channel_multiplier=0).then_inc(iotas_ready, 1)

            for i in range(2):
                pool.wait_ge(table_written[i], 16 * (NG // 2))
            pool.wait_ge(dummy_written, 16)

            def gather(b, par, S, first):
                if not first:
                    wait_apart(pool, near_used, b - 1)
                wait_apart(pool, idx_ready, b + 1)
                for s in range(S):
                    pool.indirect_dma_start(
                        out=near[par][:, s, :], out_offset=None, in_=table[:, :],
                        in_offset=bass.IndirectOffsetOnAxis(ap=idx[par][:, s:s + 1], axis=0)).then_inc(gathered[par], 16)

            for b in range(NE):
                gather(b, b % 2, slots(b), b < 2)
            with pool.Fori(NE // 2, NB // 2) as t:
                gather(2 * t, 0, SLOTS, False)
                gather(2 * t + 1, 1, SLOTS, False)

        @block.scalar
        def _(act):
            act.dma_start(w_sb[:, :], w).then_inc(params_loaded, 16)
            flat = lambda a: a.rearrange("h d -> (h d)").partition_broadcast
            act.dma_start(an_sb[:, :], flat(att_neigh)(F)).then_inc(params_loaded, 16)
            act.dma_start(as_sb[:, :], flat(att_self)(F)).then_inc(params_loaded, 16)
            act.dma_start(bias_sb[:, :], flat(bias)(P)).then_inc(params_loaded, 16)
            for i in range(2):
                act.dma_start(x_in[:, i, :, :], x_v[:, i * GB:(i + 1) * GB, :]).then_inc(xin_loaded[i], 16)
            act.dma_start(x_sb[:, :, :], x_v).then_inc(x_loaded, 16)

            def group(g, par, first, last):
                act.wait_ge(x_transposed, g + 1)
                if not first:
                    act.wait_ge(feats_ready, g - 1)
                act.activation(xt_sb[:, par, :], xt_ps[par][0:F, :], ACT.Copy).then_inc(xt_copied, 1)
                if not last:
                    act.dma_start(x_in[:, par, :, :], x_v[:, bass.ds((g + 2) * GB, GB), :]).then_inc(xin_loaded[par], 16)
                act.wait_ge(feats_copied, g + 1)
                act.dma_start(table_v[:, bass.ds(g * GB, GB), :], feat_sb[:, par, :, :]).then_inc(table_written[par], 16)

            group(0, 0, True, False)
            group(1, 1, True, False)
            with act.Fori(1, NG // 2 - 1) as t:
                group(2 * t, 0, False, False)
                group(2 * t + 1, 1, False, False)
            group(NG - 2, 0, False, True)
            group(NG - 1, 1, False, True)
            act.wait_ge(dummy_ready, 1)
            act.dma_start(table[0:1, :], dummy[:, :]).then_inc(dummy_written, 16)
            for i in range(2):
                act.wait_ge(table_written[i], 16 * (NG // 2))
            act.dma_start(nodes[:, :, :], table[1:N + 1, :].rearrange("(p j) c -> p j c", j=J)).then_inc(nodes_loaded, 16)

            def dense_loads(g):
                rows = bass.ds(g * R, R)
                act.dma_start(arow[:, :, :], adj[rows, :].rearrange("r (p j) -> p r j", j=J)).then_inc(d_loaded, 16)
                act.dma_start(own_r[:, :, :], table_r[rows, H + F:TC].partition_broadcast(P)).then_inc(d_loaded, 16)
                act.dma_start(x_r[:, :], x[rows, :]).then_inc(d_loaded, 16)

            def dense_exps(n):
                wait_apart(act, d_scores, n + 1)
                act.activation(score[:, :, :], score[:, :, :], ACT.Exp).then_inc(d_probs, 1)

            dense_loads(0)
            dense_exps(0)

            def exps(b, S):
                act.wait_ge(scores_ready, b + 1)
                act.activation(prob[:, 0:S, :], lz[:, 0:S, :], ACT.Exp).then_inc(probs_ready, 1)

            for b in range(NE):
                exps(b, slots(b))
            with act.Fori(NE, NB) as b:
                exps(b, SLOTS)
            act.wait_ge(stats_ready, 1)
            act.activation(std[:, :], rstd[:, :], ACT.Sqrt).then_inc(std_ready, 1)
            act.wait_ge(stored, 16 * STORES)

            def dense_group(g, n):
                wait_apart(act, d_out, n)
                dense_loads(g)
                dense_exps(n)
                wait_apart(act, d_var, n)
                act.activation(dstd[:, :], dvar[:, :], ACT.Sqrt).then_inc(d_std, 1)
                wait_apart(act, d_out, n + 1)
                act.dma_start(out[bass.ds(g * R, R), :], dy[:, :]).then_inc(d_stored, 16)
                wait_apart(act, d_stored, 16 * n)

            flagged_groups(act, dense_group)

        @block.tensor
        def _(pe):
            pe.wait_ge(ident_ready, 2)

            def transpose(g, par):
                pe.wait_ge(xin_loaded[par], 16 * (g // 2 + 1) if isinstance(g, int) else 8 * (g - par) + 16)
                for j in range(GB):
                    last = pe.transpose(xt_ps[par][0:F, j * P:(j + 1) * P], x_in[:, par, j, :], ident[:, :])
                last.then_inc(x_transposed, 1)

            def project(g, par, first):
                pe.wait_ge(xt_copied, g + 1)
                if not first:
                    pe.wait_ge(feats_copied, g - 1)
                for j in range(GB):
                    last = pe.matmul(ft_ps[par][:, j * TC:(j + 1) * TC], xt_sb[:, par, j * P:(j + 1) * P], wa[:, :],
                                     start=True, stop=True)
                last.then_inc(feats_ready, 1)

            transpose(0, 0)
            pe.wait_ge(wa_ready, 1)
            transpose(1, 1)
            project(0, 0, True)
            project(1, 1, True)
            with pe.Fori(1, NG // 2) as t:
                wait_apart(pe, xin_loaded[0], 16 * t + 16)
                for j in range(GB):
                    last = pe.transpose(xt_ps[0][0:F, j * P:(j + 1) * P], x_in[:, 0, j, :], ident[:, :])
                last.then_inc(x_transposed, 1)
                wait_apart(pe, xin_loaded[1], 16 * t + 16)
                for j in range(GB):
                    last = pe.transpose(xt_ps[1][0:F, j * P:(j + 1) * P], x_in[:, 1, j, :], ident[:, :])
                last.then_inc(x_transposed, 1)
                project(2 * t, 0, False)
                project(2 * t + 1, 1, False)

            pe.wait_ge(xsum_ready, 1)
            pe.matmul(mean_ps[0:F, 0:1], xsum[:, :], mean_col[:, :], start=True, stop=True).then_inc(xmean_made, 1)
            pe.wait_ge(xmean_copied, 1)
            pe.matmul(mean_ps[0:1, 0:TC], xmean[:, :], wa[:, :], start=True, stop=True).then_inc(dummy_made, 1)

            pe.wait_ge(consts_ready, 1)

            def pack(b, t, par, first):
                if not first:
                    pe.wait_ge(codes_read, b - 1)
                for h in range(2):
                    pe.wait_ge(adj_loaded[2 * par + h], 16 * t + 16)
                    for k in range(BITS // 2):
                        kk = h * BITS // 2 + k
                        last = pe.matmul(codes[par][:, :], weights[:, kk, :],
                                         adj_bf[2 * par + h][:, k * GC:(k + 1) * GC, 1],
                                         start=(kk == 0), stop=(kk == BITS - 1))
                    last.then_inc(halves_packed, 1)

            pack(0, 0, 0, True)
            pack(1, 0, 1, True)

            def dense_group(g, n):
                wait_apart(pe, d_max, n + 1)
                pe.transpose(xt_ps[0][:, 0:R * H], dmax[:, :], ident[:, :]).then_inc(d_max_t, 1)
                wait_apart(pe, d_max_col, n + 1)
                pe.transpose(xt_ps[1][:, 0:R * H], dtile[:, :], ident[:, :]).then_inc(d_max_row, 1)
                wait_apart(pe, d_probs, n + 1)
                for j in range(J):
                    last = pe.matmul(ft_ps[0][:, 0:F + 1], score[:, j, :], nodes[:, j, H:H + F + 1],
                                     start=(j == 0), stop=(j == J - 1))
                last.then_inc(d_sums, 1)
                wait_apart(pe, d_scaled, n + 1)
                pe.matmul(ft_ps[1][0:R, 0:F], row_sel[:, :], dnum[:, :], start=True, stop=True).then_inc(d_rows, 1)

            dense_group(0, 0)
            with pe.Fori(1, NB // 2) as t:
                pack(2 * t, t, 0, False)
                pack(2 * t + 1, t, 1, False)
            pe.wait_ge(over_ready, 1)
            for q in range(P // R):
                last = pe.matmul(flag_ps[0:1, q * NB:(q + 1) * NB], group_sel[:, q:q + 1], over[:, :],
                                 start=True, stop=True)
            last.then_inc(groups_summed, 1)
            flagged_groups(pe, dense_group)

        @block.vector
        def _(dve):
            chain = {"n": 0}

            def step(ins):
                chain["n"] += 1
                ins.then_inc(dve_done, 1)
                dve.wait_ge(dve_done, chain["n"])

            def clear():
                dve.sem_clear(dve_done)
                chain["n"] = 0

            dve.wait_ge(params_loaded, 64)
            wv = w_sb[:, :].rearrange("f (h d) -> f h d", d=D)
            for a_sb, o in ((an_sb, 0), (as_sb, H + F)):
                step(dve.tensor_tensor(wtmp[:, :], w_sb[:, :], a_sb[:, :], ALU.mult))
                step(dve.tensor_reduce(wa[:, o:o + H], wtmp[:, :].rearrange("f (h d) -> f h d", d=D), AX.X, ALU.add))
            dve.tensor_copy(wa[:, H:H + F], w_sb[:, :]).then_inc(wa_ready, 1)
            dve.wait_ge(iotas_ready, 2)
            dve.wait_ge(ident_ready, 2)
            step(dve.memset(one_i[:, :], 1))
            step(dve.tensor_tensor(pow_i[:, :], one_i[:, :], bit_i[:, :], ALU.logical_shift_left))
            step(dve.tensor_copy(pow_f[:, :], pow_i[:, :]))
            dve.tensor_copy(off_f[:, :], off_i[:, :])
            dve.tensor_tensor(weights[:, :, :], ident[:, :].unsqueeze(1).to_broadcast([P, BITS, P]),
                              pow_f[:, :].unsqueeze(2).to_broadcast([P, BITS, P]), ALU.mult).then_inc(consts_ready, 1)
            dve.memset(mean_col[:, :], 1.0 / N)
            step(dve.tensor_reduce(head8[:, :], ident[:, :].rearrange("p (r h) -> p h r", h=H), AX.X, ALU.add))
            dve.tensor_copy(head_mask[:, :].rearrange("p (h d) -> p h d", d=D), head8[:, :].unsqueeze(2).to_broadcast([P, H, D]))
            dve.tensor_reduce(row_sel[:, :], ident[:, :].rearrange("p (r h) -> p r h", h=H), AX.X, ALU.add)
            dve.tensor_reduce(group_sel[:, :], ident[:, :].rearrange("p (q r) -> p q r", r=R), AX.X, ALU.add)
            dve.wait_ge(x_loaded, 16)
            dve.tensor_reduce(xsum[:, :], x_sb[:, :, :].rearrange("p b f -> p f b"), AX.X, ALU.add).then_inc(xsum_ready, 1)

            def node_copy(g, t, par, first):
                dve.wait_ge(feats_ready, g + 1)
                if not first:
                    dve.wait_ge(table_written[par], 16 * t)
                fv = ft_ps[par][:, :].rearrange("p (j c) -> p j c", c=TC)
                dve.tensor_copy(feat_sb[:, par, :, :], fv)
                dve.tensor_copy(own[:, bass.ds(g * GB, GB), :], fv[:, :, H + F:TC]).then_inc(feats_copied, 1)

            node_copy(0, 0, 0, True)
            node_copy(1, 0, 1, True)
            with dve.Fori(1, NG // 2) as t:
                node_copy(2 * t, t, 0, False)
                node_copy(2 * t + 1, t, 1, False)
            dve.wait_ge(xmean_made, 1)
            dve.tensor_copy(xmean[:, :], mean_ps[0:F, 0:1]).then_inc(xmean_copied, 1)
            dve.wait_ge(dummy_made, 1)
            step(dve.tensor_copy(dummy[:, :], mean_ps[0:1, 0:TC]))
            dve.memset(dummy[:, 0:H], FAR).then_inc(dummy_ready, 1)

            def extract(b, par, S):
                R = S // 8
                wait_apart(dve, halves_packed, 2 * b + 2)
                src = codes[par][:, :]
                for r in range(R):
                    o = slice(8 * r, 8 * r + 8)
                    step(dve.max(val[:, o], src))
                    if r == R - 1:
                        step(dve.max_index(col[:, o], val[:, o], src))
                        continue
                    step(dve.max_index(col[:, o], val[:, o], src))
                    ins = dve.match_replace(work[:, :], val[:, o], src, 0.0)
                    if r == 0:
                        ins.then_inc(codes_read, 1)
                        wait_apart(dve, codes_read, b + 1)
                    else:
                        step(ins)
                    src = work[:, :]
                full = [P, S, BITS]
                step(dve.tensor_copy(val_i[:, 0:S], val[:, 0:S]))
                step(dve.tensor_tensor(hit[:, 0:S, :], val_i[:, 0:S].unsqueeze(2).to_broadcast(full),
                                       pow_i[:, :].unsqueeze(1).to_broadcast(full), ALU.bitwise_and))
                step(dve.tensor_tensor(keys[:, 0:S, :], col[:, 0:S].unsqueeze(2).to_broadcast(full),
                                       off_f[:, :].unsqueeze(1).to_broadcast(full), ALU.add))
                kv = keys[:, 0:S, :].rearrange("p s k -> p (s k)")
                step(dve.scalar_tensor_tensor(kv, hit[:, 0:S, :].rearrange("p s k -> p (s k)"), 0.0, kv, ALU.is_gt, ALU.mult))
                for r in range(R):
                    o = slice(8 * r, 8 * r + 8)
                    step(dve.max(key[:, o], kv))
                    if r < R - 1:
                        step(dve.match_replace(kv, key[:, o], kv, 0.0))
                dve.tensor_copy(idx[par][:, 0:S], key[:, 0:S]).then_inc(idx_ready, 1)
                dve.tensor_tensor(over[:, bass.ds(b, 1)], val[:, S - 1:S], key[:, S - 1:S], ALU.max)

            def scores(b, par, S, total):
                dve.wait_ge(gathered[par], 16 * total)
                g = near[par]
                step(dve.tensor_tensor(z[:, 0:S, :], g[:, 0:S, 0:H], own[:, bass.ds(b, 1), :].to_broadcast([P, S, H]), ALU.add))
                zf, lf = (a[:, 0:S, :].rearrange("p s h -> p (s h)") for a in (z, lz))
                step(dve.scalar_tensor_tensor(lf, zf, SLOPE, zf, ALU.mult, ALU.max))
                step(dve.tensor_reduce(top[:, :], lz[:, 0:S, :].rearrange("p s h -> p h s"), AX.X, ALU.max))
                dve.tensor_tensor(lz[:, 0:S, :], lz[:, 0:S, :], top[:, :].unsqueeze(1).to_broadcast([P, S, H]),
                                  ALU.subtract).then_inc(scores_ready, 1)

            def combine(b, par, S):
                g = near[par]
                dve.wait_ge(probs_ready, b + 1)
                dve.tensor_reduce(den[:, :], prob[:, 0:S, :].rearrange("p s h -> p h s"), AX.X, ALU.add)
                feat = g[:, 0:S, H:H + F]
                f4 = feat.rearrange("p s (h d) -> p s h d", d=D)
                step(dve.tensor_tensor(f4, f4, prob[:, 0:S, :].unsqueeze(3).to_broadcast([P, S, H, D]), ALU.mult))
                num_ins = dve.tensor_reduce(num[:, :], feat.rearrange("p s f -> p f s"), AX.X, ALU.add)
                num_ins.then_inc(near_used, 1)
                dve.wait_ge(near_used, b + 1)
                step(dve.reciprocal(rden[:, :], den[:, :]))
                step(dve.tensor_tensor(att[:, :].rearrange("p (h d) -> p h d", d=D), num[:, :].rearrange("p (h d) -> p h d", d=D),
                                       rden[:, :].unsqueeze(2).to_broadcast([P, H, D]), ALU.mult))
                step(dve.tensor_tensor(att[:, :], att[:, :], bias_sb[:, :], ALU.add))
                xb = x_sb[:, bass.ds(b, 1), :].rearrange("p a f -> p (a f)")
                step(dve.scalar_tensor_tensor(y[:, :], att[:, :], 0.0, xb, ALU.max, ALU.add))
                dve.tensor_copy(xb, y[:, :])
                step(dve.bn_stats(bn6[:, :], y[:, :]))
                step(dve.bn_aggr(mv[:, :], bn6[:, :]))
                step(dve.tensor_copy(stats[:, bass.ds(b, 1), :].rearrange("p a f -> p (a f)"), mv[:, :]))

            def block_step(b, par, S, total, nxt):
                clear()
                scores(b, par, S, total)
                if nxt is not None:
                    extract(b + 2, par, nxt)
                combine(b, par, S)

            def dense_rows(n):
                clear()
                wait_apart(dve, d_loaded, 48 * n + 48)
                full = [P, J, R, H]
                s4 = score[:, :, :].rearrange("p j (r h) -> p j r h", h=H)
                sf = score[:, :, :].rearrange("p j k -> p (j k)")
                step(dve.tensor_tensor(s4, nodes[:, :, 0:H].unsqueeze(2).to_broadcast(full),
                                       own_r[:, :, :].unsqueeze(1).to_broadcast(full), ALU.add))
                step(dve.scalar_tensor_tensor(sf, sf, SLOPE, sf, ALU.mult, ALU.max))
                step(dve.tensor_scalar(arow[:, :, :], arow[:, :, :], -1.0, 1e10, ALU.add, ALU.mult))
                step(dve.tensor_tensor(s4, s4, arow[:, :, :].rearrange("p r j -> p j r").unsqueeze(3).to_broadcast(full), ALU.add))
                dve.tensor_reduce(dmax[:, :], score[:, :, :].rearrange("p j k -> p k j"), AX.X, ALU.max).then_inc(d_max, 1)
                wait_apart(dve, d_max_t, n + 1)
                step(dve.tensor_reduce(dcol[:, :], xt_ps[0][:, 0:R * H], AX.X, ALU.max))
                dve.tensor_copy(dtile[:, :], dcol[:, :].to_broadcast([P, R * H])).then_inc(d_max_col, 1)
                wait_apart(dve, d_max_row, n + 1)
                dve.tensor_tensor(score[:, :, :], score[:, :, :], xt_ps[1][:, 0:R * H].unsqueeze(1).to_broadcast([P, J, R * H]),
                                  ALU.subtract).then_inc(d_scores, 1)
                wait_apart(dve, d_sums, n + 1)
                step(dve.reciprocal(drden[:, :], ft_ps[0][:, F:F + 1]))
                dve.scalar_tensor_tensor(dnum[:, :], ft_ps[0][:, 0:F], drden[:, :], head_mask[:, :], ALU.mult, ALU.mult).then_inc(d_scaled, 1)
                wait_apart(dve, d_rows, n + 1)
                step(dve.tensor_tensor(datt[:, :], ft_ps[1][0:R, 0:F], bias_sb[0:R, :], ALU.add))
                step(dve.scalar_tensor_tensor(dy[:, :], datt[:, :], 0.0, x_r[:, :], ALU.max, ALU.add))
                step(dve.bn_stats(dbn6[:, :], dy[:, :]))
                step(dve.bn_aggr(dmv[:, :], dbn6[:, :]))

            extract(0, 0, slots(0))
            extract(1, 1, slots(1))
            dve.wait_ge(nodes_loaded, 16)
            dve.memset(nodes[:, :, H + F:H + F + 1], 1.0)
            dense_rows(0)
            total = [0, 0]
            for b in range(NE):
                total[b % 2] += slots(b)
                block_step(b, b % 2, slots(b), total[b % 2], slots(b + 2))
                if b == 0:
                    dve.tensor_copy(x_sb[0:R, 0, :], dy[:, :])
                    dve.tensor_copy(stats[0:R, 0, :], dmv[:, :])
                    dve.memset(over[0:R, 0:1], 0.0).then_inc(d_out, 1)
            T = (NB - NE) // 2 - 1
            with dve.Fori(0, T) as t:
                for par in range(2):
                    block_step(NE + 2 * t + par, par, SLOTS, total[par] + (t + 1) * SLOTS, SLOTS)
            for par in range(2):
                block_step(NB - 2 + par, par, SLOTS, total[par] + (T + 1) * SLOTS, None)

            dve.sem_inc(over_ready, 1)
            step(dve.tensor_scalar(rstd[:, :], stats[:, :, 1], EPS, None, ALU.add))
            dve.sem_inc(stats_ready, 1)
            dve.wait_ge(std_ready, 1)
            step(dve.reciprocal(rstd[:, :], std[:, :]))
            for c in range(STORES):
                o = slice(c * CH, (c + 1) * CH)
                full = [P, CH, F]
                step(dve.tensor_tensor(x_sb[:, o, :], x_sb[:, o, :], stats[:, o, 0].unsqueeze(2).to_broadcast(full), ALU.subtract))
                dve.tensor_tensor(x_sb[:, o, :], x_sb[:, o, :], rstd[:, o].unsqueeze(2).to_broadcast(full), ALU.mult).then_inc(out_ready, 1)

            dve.wait_ge(groups_summed, 1)
            clear()
            step(dve.memset(gzero, 0.0))
            step(dve.tensor_scalar(gflag_f[:, :, :], flag_ps[:, :].rearrange("o (q b) -> o b q", b=NB), 0.0, None, ALU.is_gt))
            gf = gflag_f[:, :, :].rearrange("o b q -> o (b q)")
            step(dve.tensor_tensor_scan(gcount, gf, gzero, 1.0, ALU.add, ALU.add))
            step(dve.tensor_tensor(gturn[:, :], gcount, gf, ALU.subtract))
            step(dve.tensor_copy(gflag[:, :], gf))
            step(dve.tensor_reduce(bflag_f[:, :], gflag_f[:, :, :], AX.X, ALU.max))
            dve.tensor_copy(bflag[:, :], bflag_f[:, :]).then_inc(flags_ready, 1)

            def dense_group(g, n):
                dense_rows(n)
                dve.tensor_scalar(dvar[:, :], dmv[:, 1:2], EPS, None, ALU.add).then_inc(d_var, 1)
                wait_apart(dve, d_std, n)
                step(dve.reciprocal(drstd[:, :], dstd[:, :]))
                dve.tensor_scalar(dy[:, :], dy[:, :], dmv[:, 0:1], drstd[:, :], ALU.subtract, ALU.mult).then_inc(d_out, 1)

            flagged_groups(dve, dense_group)


_INS = ["x", "adj", "L0_gnn_W", "L0_gnn_att_self", "L0_gnn_att_neigh", "L0_gnn_bias"]


def kernel(**inputs):
    import numpy as _np
    import concourse.bacc as _bacc
    from concourse import mybir as _mybir
    from concourse.bass_utils import run_bass_kernel_spmd as _run

    nc = _bacc.Bacc("TRN2", target_bir_lowering=False, num_devices=1)
    arrays, args = {}, []
    for name in _INS:
        a = _np.ascontiguousarray(inputs[name])
        arrays[f"in_{name}_dram"] = a
        args.append(nc.dram_tensor(f"in_{name}_dram", a.shape, _mybir.dt.from_np(a.dtype), kind="ExternalInput").ap())
    out = nc.dram_tensor("out_dram", inputs["x"].shape, _mybir.dt.float32, kind="ExternalOutput").ap()
    gat_resnorm(nc, *args, out)
    r = _run(nc, [arrays], core_ids=[0])
    return r.results[0]["out_dram"]
```

```python
import concourse.bass as bass
from concourse import mybir
from contextlib import ExitStack


def gat_resnorm(nc, x, adj, w, att_self, att_neigh, bias, out):
    fp32, bf16 = mybir.dt.float32, mybir.dt.bfloat16
    i32, u32 = mybir.dt.int32, mybir.dt.uint32
    ALU, ACT, AX = mybir.AluOpType, mybir.ActivationFunctionType, mybir.AxisListType

    N, F = x.shape
    H, D = att_self.shape
    P = 128
    NB = N // P
    BITS = 16
    GC = N // BITS
    HALF = N // 2
    TC = 2 * H + F
    GB = 4
    NG = NB // GB
    SLOPE = 0.2
    EPS = 1e-5
    FAR = -1e30
    R = 16
    J = N // P
    GPB = P // R
    NGR = N // R
    EARLY = [56] + [32] * 7
    SLOTS = 16
    PAST = 1e5
    RING = 4
    AHEAD = 3
    XC = 4
    STORES = 4
    CH = NB // STORES
    PB = 512
    S_MAX = max(EARLY)
    NE = len(EARLY)

    LATE = 2

    def plan(b):
        return (EARLY[b], 8) if isinstance(b, int) and b < NE else (SLOTS, 6)

    ctx = ExitStack()
    with ctx:
        def sb(name, shape, dt):
            return ctx.enter_context(nc.sbuf_tensor(name, shape, dt))

        def pb(name, shape, dt):
            return ctx.enter_context(nc.psum_tensor(name, shape, dt))

        def sem(name):
            return ctx.enter_context(nc.semaphore(name))

        table = nc.dram_tensor("node_table", [N + 1, TC], fp32)

        adj_sb = sb("adj_sb", [P, 4, HALF], fp32)
        x_sb = sb("x_sb", [P, NB, F], fp32)
        own = sb("own", [P, NB, H], fp32)
        w_sb = sb("w_sb", [F, F], fp32)
        an_sb = sb("an_sb", [F, F], fp32)
        as_sb = sb("as_sb", [F, F], fp32)
        wtmp = sb("wtmp", [F, F], fp32)
        wa = sb("wa", [F, TC], fp32)
        bias_sb = sb("bias_sb", [P, F], fp32)
        ident = sb("ident", [P, P], fp32)
        weights = sb("weights", [P, BITS, P], bf16)
        ones = sb("ones", [P, 1], fp32)
        one_i = sb("one_i", [P, BITS], i32)
        bit_i = sb("bit_i", [P, BITS], i32)
        pow_i = sb("pow_i", [P, BITS], i32)
        pow_f = sb("pow_f", [P, BITS], fp32)
        off_i = sb("off_i", [P, BITS], i32)
        off_f = sb("off_f", [P, BITS], fp32)
        work = sb("work", [P, GC], fp32)
        val = sb("val", [P, S_MAX], fp32)
        col = sb("col", [P, S_MAX], u32)
        val_i = sb("val_i", [P, S_MAX], i32)
        hit = sb("hit", [P, S_MAX, BITS], i32)
        keys = sb("keys", [P, S_MAX, BITS], fp32)
        key = [sb(f"key{i}", [P, S_MAX], fp32) for i in range(RING)]
        absent = [sb(f"absent{i}", [P, S_MAX], fp32) for i in range(RING)]
        idx = [sb(f"idx{i}", [P, S_MAX], u32) for i in range(RING)]
        sign = sb("sign", [1, S_MAX], fp32)
        count_f = sb("count_f", [1, RING], fp32)
        count_i = sb("count_i", [1, RING], i32)
        over = sb("over", [P, NB], fp32)
        near = [sb(f"near{i}", [P, n, TC], fp32) for i, n in enumerate((S_MAX, max(EARLY[1:])))]
        z = sb("z", [P, S_MAX, H], fp32)
        lz = sb("lz", [P, S_MAX, H], fp32)
        top = sb("top", [P, H], fp32)
        rden = sb("rden", [P, RING, H], fp32)
        att = sb("att", [P, RING, F], fp32)
        bn6 = sb("bn6", [P, RING, 6], fp32)
        mv = sb("mv", [P, RING, 2], fp32)
        stats = sb("stats", [P, NB, 2], fp32)
        var = sb("var", [P, NB], fp32)
        std = sb("std", [P, NB], fp32)
        rstd = sb("rstd", [P, NB], fp32)
        nodes = sb("nodes", [P, J, TC], fp32)
        score = sb("score", [P, J, R * H], fp32)
        spare = score[:, :, :].rearrange("p j k -> p (j k)")
        n_xt, n_ft = 2 * GB * P, NB * TC
        xt_sb = spare[0:F, 0:n_xt].rearrange("p (i c) -> p i c", i=2)
        feat_sb = spare[:, n_xt:n_xt + n_ft].rearrange("p (b c) -> p b c", c=TC)
        arow = sb("arow", [P, R, J], fp32)
        own_r = sb("own_r", [P, R, H], fp32)
        x_r = sb("x_r", [R, F], fp32)
        dmax = sb("dmax", [P, R * H], fp32)
        dcol = sb("dcol", [P, 1], fp32)
        dtile = sb("dtile", [P, R * H], fp32)
        drden = sb("drden", [P, 1], fp32)
        dnum = sb("dnum", [P, F], fp32)
        datt = sb("datt", [R, F], fp32)
        dy = sb("dy", [R, F], fp32)
        dbn6 = sb("dbn6", [R, 6], fp32)
        dmv = sb("dmv", [R, 2], fp32)
        dvar = sb("dvar", [R, 1], fp32)
        dstd = sb("dstd", [R, 1], fp32)
        drstd = sb("drstd", [R, 1], fp32)
        head8 = sb("head8", [P, H], fp32)
        head_mask = sb("head_mask", [P, F], fp32)
        row_sel = sb("row_sel", [P, R], fp32)
        group_sel = sb("group_sel", [P, GPB], fp32)
        gflag_f = hit[0:1, 0:NGR // BITS, :].rearrange("o s k -> o (s k)").bitcast(fp32)
        gcount = keys[0:1, 0:NGR // BITS, :].rearrange("o s k -> o (s k)")
        gzero = work[0:1, 0:NGR]
        gflag = sb("gflag", [1, NGR], i32)
        gturn = sb("gturn", [1, NGR], i32)
        bflag = sb("bflag", [1, NB], i32)
        bflag_f = sb("bflag_f", [1, NB], fp32)
        aflag = sb("aflag", [1, 1], i32)

        codes = [pb(f"codes{i}", [P, GC], fp32) for i in range(RING)]
        xt_ps = [pb(f"xt_ps{i}", [P, GB * P], fp32) for i in range(2)]
        ft_ps = [pb(f"ft_ps{i}", [P, PB], fp32) for i in range(2)]
        sums_ps = xt_ps[1][:, 0:RING * (H + F)]
        count_ps = [ft_ps[1][0:1, P + i * S_MAX:P + (i + 1) * S_MAX] for i in range(RING)]
        max_ps = xt_ps[0][:, 0:R * H]
        maxrow_ps = xt_ps[0][:, R * H:2 * R * H]
        dsum_ps = ft_ps[0][:, 0:F + 1]
        drow_ps = ft_ps[1][0:R, 0:F]
        flag_ps = codes[0][0:1, 0:NGR]

        params_loaded = sem("params_loaded")
        x_loaded = [sem(f"x_loaded{i}") for i in range(XC)]
        adj_loaded = [sem(f"adj_loaded{i}") for i in range(4)]
        ident_ready = sem("ident_ready")
        iotas_ready = sem("iotas_ready")
        near_zeroed = sem("near_zeroed")
        ones_ready = sem("ones_ready")
        dve_done = sem("dve_done")
        weights_ready = sem("weights_ready")
        wa_ready = sem("wa_ready")
        x_transposed = sem("x_transposed")
        xt_copied = sem("xt_copied")
        feats_ready = sem("feats_ready")
        feats_copied = sem("feats_copied")
        table_written = sem("table_written")
        nodes_loaded = sem("nodes_loaded")
        halves_packed = sem("halves_packed")
        codes_read = sem("codes_read")
        keys_ready = sem("keys_ready")
        keys_counted = sem("keys_counted")
        signs_summed = sem("signs_summed")
        count_ready = sem("count_ready")
        idx_ready = sem("idx_ready")
        gathered = [sem(f"gathered{i}") for i in range(2)]
        rows_ready = sem("rows_ready")
        scores_ready = sem("scores_ready")
        probs_ready = sem("probs_ready")
        products_ready = sem("products_ready")
        slots_summed = sem("slots_summed")
        var_ready = sem("var_ready")
        std_ready = sem("std_ready")
        out_ready = sem("out_ready")
        stored = sem("stored")
        over_ready = sem("over_ready")
        groups_summed = sem("groups_summed")
        flags_ready = sem("flags_ready")
        d_loaded = sem("d_loaded")
        d_max = sem("d_max")
        d_max_t = sem("d_max_t")
        d_max_col = sem("d_max_col")
        d_max_row = sem("d_max_row")
        d_scores = sem("d_scores")
        d_probs = sem("d_probs")
        d_sums = sem("d_sums")
        d_scaled = sem("d_scaled")
        d_rows = sem("d_rows")
        d_var = sem("d_var")
        d_std = sem("d_std")
        d_out = sem("d_out")
        d_stored = sem("d_stored")
        waits_passed = sem("waits_passed")

        adj_v = adj.rearrange("(b p) (h c) -> b p h c", p=P, h=2)
        x_v = x.rearrange("(b p) f -> p b f", p=P)
        out_v = out.rearrange("(b p) f -> p b f", p=P)
        table_r = table[1:N + 1, :]
        table_v = table_r.rearrange("(b p) c -> p b c", p=P)
        adj_bf = [adj_sb[:, q, :].bitcast(bf16).rearrange("p (c two) -> p c two", two=2) for q in range(4)]

        def wait_apart(eng, signal, value):
            eng.wait_ge(signal, value)
            eng.sem_inc(waits_passed, 1)

        def every_block(eng, turn):
            for b in range(NE):
                turn(b, b % RING, False)
            with eng.Fori(NE // RING, NB // RING - 1) as t:
                for i in range(RING):
                    turn(RING * t + i, i, False)
            for b in range(NB - RING, NB):
                turn(b, b % RING, True)

        def flagged_groups(eng, body):
            eng.wait_ge(flags_ready, 1)
            any_at_all = eng.value_load(aflag[0:1, 0:1], min_val=0, max_val=1)
            with eng.If(any_at_all > 0):
                with eng.Fori(0, NB) as b:
                    any_group = eng.value_load(bflag[0:1, bass.ds(b, 1)], min_val=0, max_val=1)
                    with eng.If(any_group > 0):
                        with eng.Fori(0, GPB) as q:
                            g = b * GPB + q
                            this_group = eng.value_load(gflag[0:1, bass.ds(g, 1)], min_val=0, max_val=1)
                            with eng.If(this_group > 0):
                                turn = eng.value_load(gturn[0:1, bass.ds(g, 1)], min_val=1, max_val=NGR)
                                body(g, turn)

        block = ctx.enter_context(nc.Block())

        @block.sync
        def _(sp):
            for c in range(XC):
                o = slice(c * NB // XC, (c + 1) * NB // XC)
                sp.dma_start(x_sb[:, o, :], x_v[:, o, :]).then_inc(x_loaded[c], 16)

            def load(b, par, first):
                for h in range(2):
                    if not first:
                        sp.wait_ge(halves_packed, 2 * b - 3 + h)
                    sp.dma_start(adj_sb[:, 2 * par + h, :], adj_v[b, :, h, :]).then_inc(adj_loaded[2 * par + h], 16)

            load(0, 0, True)
            load(1, 1, True)
            with sp.Fori(1, NB // 2) as t:
                load(2 * t, 0, False)
                load(2 * t + 1, 1, False)
            for c in range(STORES):
                sp.wait_ge(out_ready, c + 1)
                sp.dma_start(out_v[:, c * CH:(c + 1) * CH, :], x_sb[:, c * CH:(c + 1) * CH, :]).then_inc(stored, 16)
            sp.wait_ge(stored, 16 * STORES)

        @block.gpsimd
        def _(pool):
            pool.memset(ident[:, :], 0.0).then_inc(ident_ready, 1)
            pool.wait_ge(ident_ready, 1)
            pool.affine_select(out=ident[:, :], in_=ident[:, :], compare_op=ALU.not_equal, fill=1.0,
                               base=0, pattern=[[-1, P]], channel_multiplier=1).then_inc(ident_ready, 1)
            pool.iota(bit_i[:, :], [[1, BITS]], base=0, channel_multiplier=0).then_inc(iotas_ready, 1)
            pool.iota(off_i[:, :], [[GC, BITS]], base=1, channel_multiplier=0).then_inc(iotas_ready, 1)
            pool.memset(ones[:, :], 1.0).then_inc(ones_ready, 1)
            for i in range(2):
                pool.memset(near[i][:, :, :], 0.0).then_inc(near_zeroed, 1)

            pool.wait_ge(table_written, 16 * (XC + 1))
            pool.wait_ge(near_zeroed, 2)

            issued = [pool.alloc_register(f"issued{i}") for i in range(2)]
            for i in range(2):
                pool.reg_mov(issued[i], 0)

            def rows_arrived(par):
                wait_apart(pool, gathered[par], pool.snap(issued[par]))
                pool.sem_inc(rows_ready, 1)

            def gather(b, i, tail):
                S, first = plan(b)
                par = i % 2
                wait_apart(pool, idx_ready, b + 1)
                wait_apart(pool, count_ready, b + 1)
                count = pool.value_load(count_i[0:1, i:i + 1], min_val=0, max_val=S_MAX)
                if not isinstance(b, int) or b >= 2:
                    wait_apart(pool, slots_summed, b - 1)

                def slot(k):
                    pool.indirect_dma_start(
                        out=near[par][:, k, :], out_offset=None, in_=table[:, :],
                        in_offset=bass.IndirectOffsetOnAxis(ap=idx[i][:, k:k + 1], axis=0),
                        bounds_check=N, oob_is_err=False).then_inc(gathered[par], 16)

                def slots_behind(k):
                    if k == S:
                        pool.reg_add(issued[par], issued[par], 16 * k)
                        return
                    with pool.If(count > k):
                        slot(k)
                        slots_behind(k + 1)
                    with pool.Else():
                        pool.reg_add(issued[par], issued[par], 16 * k)

                for k in range(first):
                    slot(k)
                    if k == LATE and not (isinstance(b, int) and b == 0):
                        rows_arrived(1 - par)
                slots_behind(first)

            every_block(pool, gather)
            rows_arrived((NB - 1) % 2)

        @block.scalar
        def _(act):
            act.dma_start(w_sb[:, :], w).then_inc(params_loaded, 16)

            def flat(a, n):
                return a.rearrange("h d -> (h d)").partition_broadcast(n)

            act.dma_start(an_sb[:, :], flat(att_neigh, F)).then_inc(params_loaded, 16)
            act.dma_start(as_sb[:, :], flat(att_self, F)).then_inc(params_loaded, 16)
            act.dma_start(bias_sb[:, :], flat(bias, P)).then_inc(params_loaded, 16)
            for g in range(NG + 1):
                if g < NG:
                    act.wait_ge(x_transposed, g + 1)
                    if g >= 2:
                        act.wait_ge(feats_ready, g - 1)
                    act.activation(xt_sb[:, g % 2, :], xt_ps[g % 2][0:F, :], ACT.Copy).then_inc(xt_copied, 1)
                if g > 0:
                    q = g - 1
                    act.wait_ge(feats_ready, q + 1)
                    fv = ft_ps[q % 2][:, 0:GB * TC].rearrange("p (j c) -> p j c", c=TC)
                    o = slice(q * GB, (q + 1) * GB)
                    act.activation(own[:, o, :], fv[:, :, H + F:TC], ACT.Copy)
                    act.activation(feat_sb[:, o, :], fv, ACT.Copy).then_inc(feats_copied, 1)
                    if (q + 1) % (NG // XC) == 0:
                        o = slice((q + 1 - NG // XC) * GB, (q + 1) * GB)
                        act.wait_ge(feats_copied, q + 1)
                        act.dma_start(table_v[:, o, :], feat_sb[:, o, :]).then_inc(table_written, 16)
            act.dma_start(table[0:1, :], feat_sb[0:1, 0, :]).then_inc(table_written, 16)

            def count_slots(b, i):
                S = plan(b)[0]
                wait_apart(act, keys_counted, b + 1)
                act.activation(sign[:, 0:S], count_ps[i][:, 0:S], ACT.Sign, accum_out=count_f[:, i:i + 1]).then_inc(signs_summed, 1)
                wait_apart(act, signs_summed, b + 1)
                act.activation(count_i[:, i:i + 1], count_f[:, i:i + 1], ACT.Copy).then_inc(count_ready, 1)

            for b in range(AHEAD):
                count_slots(b, b)

            act.wait_ge(table_written, 16 * (XC + 1))
            act.dma_start(nodes[:, :, :], table_r.rearrange("(p j) c -> p j c", j=J)).then_inc(nodes_loaded, 16)

            def dense_loads(g):
                rows = bass.ds(g * R, R)
                act.dma_start(arow[:, :, :], adj[rows, :].rearrange("r (p j) -> p r j", j=J)).then_inc(d_loaded, 16)
                act.dma_start(own_r[:, :, :], table_r[rows, H + F:TC].partition_broadcast(P)).then_inc(d_loaded, 16)
                act.dma_start(x_r[:, :], x[rows, :]).then_inc(d_loaded, 16)

            def dense_exps(n):
                wait_apart(act, d_scores, n + 1)
                act.activation(score[:, :, :], score[:, :, :], ACT.Exp).then_inc(d_probs, 1)

            dense_loads(0)
            dense_exps(0)

            def turn(b, i, tail):
                S = plan(b)[0]
                wait_apart(act, scores_ready, b + 1)
                act.activation(near[i % 2][:, 0:S, 0:H], lz[:, 0:S, :], ACT.Exp).then_inc(probs_ready, 1)
                if not tail or b + AHEAD < NB:
                    count_slots(b + AHEAD, (i + AHEAD) % RING)

            every_block(act, turn)
            act.wait_ge(var_ready, 1)
            act.activation(std[:, :], var[:, :], ACT.Sqrt).then_inc(std_ready, 1)
            act.wait_ge(stored, 16 * STORES)

            def dense_group(g, n):
                wait_apart(act, d_out, n)
                dense_loads(g)
                dense_exps(n)
                wait_apart(act, d_var, n)
                act.activation(dstd[:, :], dvar[:, :], ACT.Sqrt).then_inc(d_std, 1)
                wait_apart(act, d_out, n + 1)
                act.dma_start(out[bass.ds(g * R, R), :], dy[:, :]).then_inc(d_stored, 16)
                wait_apart(act, d_stored, 16 * n)

            flagged_groups(act, dense_group)

        @block.tensor
        def _(pe):
            def transpose(g):
                if g % (NG // XC) == 0:
                    pe.wait_ge(x_loaded[g // (NG // XC)], 16)
                if g >= 2:
                    pe.wait_ge(xt_copied, g - 1)
                for j in range(GB):
                    last = pe.transpose(xt_ps[g % 2][0:F, j * P:(j + 1) * P], x_sb[:, g * GB + j, :], ident[:, :])
                last.then_inc(x_transposed, 1)

            def project(g):
                pe.wait_ge(xt_copied, g + 1)
                if g >= 2:
                    pe.wait_ge(feats_copied, g - 1)
                for j in range(GB):
                    last = pe.matmul(ft_ps[g % 2][:, j * TC:(j + 1) * TC], xt_sb[:, g % 2, j * P:(j + 1) * P], wa[:, :],
                                     start=True, stop=True)
                last.then_inc(feats_ready, 1)

            def pack(b, i):
                if not isinstance(b, int) or b >= RING:
                    wait_apart(pe, codes_read, b - 3)
                for h in range(2):
                    q = 2 * (i % 2) + h
                    wait_apart(pe, adj_loaded[q], 16 * (b // 2 + 1) if isinstance(b, int) else 8 * (b - i % 2) + 16)
                    for k in range(BITS // 2):
                        kk = h * BITS // 2 + k
                        last = pe.matmul(codes[i][:, :], weights[:, kk, :], adj_bf[q][:, k * GC:(k + 1) * GC, 1],
                                         start=(kk == 0), stop=(kk == BITS - 1))
                    last.then_inc(halves_packed, 1)

            def count_keys(b, i):
                S = plan(b)[0]
                if not isinstance(b, int) or b > 0:
                    wait_apart(pe, signs_summed, b)
                wait_apart(pe, keys_ready, b + 1)
                pe.matmul(count_ps[i][:, 0:S], ones[:, :], key[i][:, 0:S], start=True, stop=True).then_inc(keys_counted, 1)

            pe.wait_ge(ident_ready, 2)
            transpose(0)
            pe.wait_ge(wa_ready, 1)
            for g in range(NG):
                if g + 1 < NG:
                    transpose(g + 1)
                project(g)
                if g == NG // 2:
                    pe.wait_ge(weights_ready, 1)
                    pack(0, 0)
            pe.wait_ge(feats_copied, NG)
            pe.wait_ge(ones_ready, 1)
            for b in range(1, RING):
                pack(b, b)
            for b in range(AHEAD):
                count_keys(b, b)

            def dense_group(g, n):
                wait_apart(pe, d_max, n + 1)
                pe.transpose(max_ps, dmax[:, :], ident[:, :]).then_inc(d_max_t, 1)
                wait_apart(pe, d_max_col, n + 1)
                pe.transpose(maxrow_ps, dtile[:, :], ident[:, :]).then_inc(d_max_row, 1)
                wait_apart(pe, d_probs, n + 1)
                for j in range(J):
                    last = pe.matmul(dsum_ps, score[:, j, :], nodes[:, j, H:H + F + 1],
                                     start=(j == 0), stop=(j == J - 1))
                last.then_inc(d_sums, 1)
                wait_apart(pe, d_scaled, n + 1)
                pe.matmul(drow_ps, row_sel[:, :], dnum[:, :], start=True, stop=True).then_inc(d_rows, 1)

            pe.wait_ge(signs_summed, AHEAD)
            dense_group(0, 0)

            def turn(b, i, tail):
                S = plan(b)[0]
                wait_apart(pe, products_ready, b + 1)
                for s in range(S):
                    last = pe.matmul(sums_ps[:, i * (H + F):(i + 1) * (H + F)], ident[:, :], near[i % 2][:, s, 0:H + F],
                                     start=(s == 0), stop=(s == S - 1))
                last.then_inc(slots_summed, 1)
                if not tail:
                    pack(b + RING, i)
                if not tail or b + AHEAD < NB:
                    count_keys(b + AHEAD, (i + AHEAD) % RING)

            every_block(pe, turn)
            pe.wait_ge(over_ready, 1)
            for q in range(GPB):
                last = pe.matmul(flag_ps[:, q * NB:(q + 1) * NB], group_sel[:, q:q + 1], over[:, :], start=True, stop=True)
            last.then_inc(groups_summed, 1)
            flagged_groups(pe, dense_group)

        @block.vector
        def _(dve):
            chain = {"n": 0}

            def step(ins):
                chain["n"] += 1
                ins.then_inc(dve_done, 1)
                dve.wait_ge(dve_done, chain["n"])

            def clear():
                dve.sem_clear(dve_done)
                chain["n"] = 0

            dve.wait_ge(params_loaded, 64)
            for a_sb, o in ((an_sb, 0), (as_sb, H + F)):
                step(dve.tensor_tensor(wtmp[:, :], w_sb[:, :], a_sb[:, :], ALU.mult))
                step(dve.tensor_reduce(wa[:, o:o + H], wtmp[:, :].rearrange("f (h d) -> f h d", d=D), AX.X, ALU.add))
            dve.tensor_copy(wa[:, H:H + F], w_sb[:, :]).then_inc(wa_ready, 1)
            dve.wait_ge(iotas_ready, 2)
            dve.wait_ge(ident_ready, 2)
            step(dve.memset(one_i[:, :], 1))
            step(dve.tensor_tensor(pow_i[:, :], one_i[:, :], bit_i[:, :], ALU.logical_shift_left))
            step(dve.tensor_copy(pow_f[:, :], pow_i[:, :]))
            dve.tensor_copy(off_f[:, :], off_i[:, :])
            dve.tensor_tensor(weights[:, :, :], ident[:, :].unsqueeze(1).to_broadcast([P, BITS, P]),
                              pow_f[:, :].unsqueeze(2).to_broadcast([P, BITS, P]), ALU.mult).then_inc(weights_ready, 1)
            step(dve.tensor_reduce(head8[:, :], ident[:, :].rearrange("p (r h) -> p h r", h=H), AX.X, ALU.add))
            dve.tensor_copy(head_mask[:, :].rearrange("p (h d) -> p h d", d=D), head8[:, :].unsqueeze(2).to_broadcast([P, H, D]))
            dve.tensor_reduce(row_sel[:, :], ident[:, :].rearrange("p (r h) -> p r h", h=H), AX.X, ALU.add)
            dve.tensor_reduce(group_sel[:, :], ident[:, :].rearrange("p (q r) -> p q r", r=R), AX.X, ALU.add)

            def extract(b, i):
                S = plan(b)[0]
                rounds = S // 8
                wait_apart(dve, halves_packed, 2 * b + 2)
                src = codes[i][:, :]
                for r in range(rounds):
                    o = slice(8 * r, 8 * r + 8)
                    step(dve.max(val[:, o], src))
                    step(dve.max_index(col[:, o], val[:, o], src))
                    if r == rounds - 1:
                        continue
                    ins = dve.match_replace(work[:, :], val[:, o], src, 0.0)
                    if r == 0:
                        ins.then_inc(codes_read, 1)
                        wait_apart(dve, codes_read, b + 1)
                    else:
                        step(ins)
                    src = work[:, :]
                full = [P, S, BITS]
                kv, hv = (a[:, 0:S, :].rearrange("p s k -> p (s k)") for a in (keys, hit))
                step(dve.tensor_copy(val_i[:, 0:S], val[:, 0:S]))
                step(dve.tensor_tensor(hit[:, 0:S, :], val_i[:, 0:S].unsqueeze(2).to_broadcast(full),
                                       pow_i[:, :].unsqueeze(1).to_broadcast(full), ALU.bitwise_and))
                step(dve.tensor_tensor(keys[:, 0:S, :], col[:, 0:S].unsqueeze(2).to_broadcast(full),
                                       off_f[:, :].unsqueeze(1).to_broadcast(full), ALU.add))
                step(dve.scalar_tensor_tensor(kv, hv, 0.0, kv, ALU.is_gt, ALU.mult))
                for r in range(rounds):
                    o = slice(8 * r, 8 * r + 8)
                    ins = dve.max(key[i][:, o], kv)
                    if r < rounds - 1:
                        step(ins)
                        step(dve.match_replace(kv, key[i][:, o], kv, 0.0))
                ins.then_inc(keys_ready, 1)
                wait_apart(dve, keys_ready, b + 1)
                step(dve.tensor_scalar(absent[i][:, 0:S], key[i][:, 0:S], 0.0, FAR, ALU.is_equal, ALU.mult))
                dve.scalar_tensor_tensor(idx[i][:, 0:S], absent[i][:, 0:S], PAST / FAR, key[i][:, 0:S],
                                         ALU.mult, ALU.add).then_inc(idx_ready, 1)
                dve.scalar_tensor_tensor(over[:, bass.ds(b, 1)], absent[i][:, 0:1], -1.0, key[i][:, S - 1:S], ALU.mult, ALU.max)

            def scores(b, i):
                S = plan(b)[0]
                g = near[i % 2]
                full = [P, S, H]
                dve.wait_ge(rows_ready, b + 1)
                step(dve.tensor_tensor(z[:, 0:S, :], g[:, 0:S, 0:H], own[:, bass.ds(b, 1), :].to_broadcast(full), ALU.add))
                step(dve.tensor_tensor(z[:, 0:S, :], z[:, 0:S, :], absent[i][:, 0:S].unsqueeze(2).to_broadcast(full), ALU.add))
                zf, lf = (a[:, 0:S, :].rearrange("p s h -> p (s h)") for a in (z, lz))
                step(dve.scalar_tensor_tensor(lf, zf, SLOPE, zf, ALU.mult, ALU.max))
                step(dve.tensor_reduce(top[:, :], lz[:, 0:S, :].rearrange("p s h -> p h s"), AX.X, ALU.max))
                dve.tensor_tensor(lz[:, 0:S, :], lz[:, 0:S, :], top[:, :].unsqueeze(1).to_broadcast(full),
                                  ALU.subtract).then_inc(scores_ready, 1)

            def products(b, i):
                S = plan(b)[0]
                g = near[i % 2]
                feat = g[:, 0:S, H:H + F].rearrange("p s (h d) -> p s h d", d=D)
                dve.wait_ge(probs_ready, b + 1)
                dve.tensor_tensor(feat, feat, g[:, 0:S, 0:H].unsqueeze(3).to_broadcast([P, S, H, D]),
                                  ALU.mult).then_inc(products_ready, 1)

            def finish(b0):
                sums = sums_ps.rearrange("p (i c) -> p i c", i=RING)
                dve.wait_ge(slots_summed, b0 + RING)
                step(dve.reciprocal(rden[:, :, :], sums[:, :, 0:H]))
                step(dve.tensor_tensor(att[:, :, :].rearrange("p i (h d) -> p i h d", d=D),
                                       sums[:, :, H:H + F].rearrange("p i (h d) -> p i h d", d=D),
                                       rden[:, :, :].unsqueeze(3).to_broadcast([P, RING, H, D]), ALU.mult))
                step(dve.tensor_tensor(att[:, :, :], att[:, :, :], bias_sb[:, :].unsqueeze(1).to_broadcast([P, RING, F]), ALU.add))
                af = att[:, :, :].rearrange("p i f -> p (i f)")
                xf = x_sb[:, bass.ds(b0, RING), :].rearrange("p i f -> p (i f)")
                step(dve.scalar_tensor_tensor(xf, af, 0.0, xf, ALU.max, ALU.add))
                for i in range(RING):
                    ins = dve.bn_stats(bn6[:, i, :], x_sb[:, bass.ds(b0 + i, 1), :].rearrange("p i f -> p (i f)"))
                step(ins)
                for i in range(RING):
                    ins = dve.bn_aggr(mv[:, i, :], bn6[:, i, :])
                step(ins)
                step(dve.tensor_copy(stats[:, bass.ds(b0, RING), :], mv[:, :, :]))

            def dense_rows(n):
                clear()
                wait_apart(dve, d_loaded, 48 * n + 48)
                full = [P, J, R, H]
                s4 = score[:, :, :].rearrange("p j (r h) -> p j r h", h=H)
                sf = score[:, :, :].rearrange("p j k -> p (j k)")
                step(dve.tensor_tensor(s4, nodes[:, :, 0:H].unsqueeze(2).to_broadcast(full),
                                       own_r[:, :, :].unsqueeze(1).to_broadcast(full), ALU.add))
                step(dve.scalar_tensor_tensor(sf, sf, SLOPE, sf, ALU.mult, ALU.max))
                step(dve.tensor_scalar(arow[:, :, :], arow[:, :, :], -1.0, 1e10, ALU.add, ALU.mult))
                step(dve.tensor_tensor(s4, s4, arow[:, :, :].rearrange("p r j -> p j r").unsqueeze(3).to_broadcast(full), ALU.add))
                dve.tensor_reduce(dmax[:, :], score[:, :, :].rearrange("p j k -> p k j"), AX.X, ALU.max).then_inc(d_max, 1)
                wait_apart(dve, d_max_t, n + 1)
                step(dve.tensor_reduce(dcol[:, :], max_ps, AX.X, ALU.max))
                dve.tensor_copy(dtile[:, :], dcol[:, :].to_broadcast([P, R * H])).then_inc(d_max_col, 1)
                wait_apart(dve, d_max_row, n + 1)
                dve.tensor_tensor(score[:, :, :], score[:, :, :], maxrow_ps.unsqueeze(1).to_broadcast([P, J, R * H]),
                                  ALU.subtract).then_inc(d_scores, 1)
                wait_apart(dve, d_sums, n + 1)
                step(dve.reciprocal(drden[:, :], dsum_ps[:, F:F + 1]))
                dve.scalar_tensor_tensor(dnum[:, :], dsum_ps[:, 0:F], drden[:, :], head_mask[:, :], ALU.mult, ALU.mult).then_inc(d_scaled, 1)
                wait_apart(dve, d_rows, n + 1)
                step(dve.tensor_tensor(datt[:, :], drow_ps, bias_sb[0:R, :], ALU.add))
                step(dve.scalar_tensor_tensor(dy[:, :], datt[:, :], 0.0, x_r[:, :], ALU.max, ALU.add))
                step(dve.bn_stats(dbn6[:, :], dy[:, :]))
                step(dve.bn_aggr(dmv[:, :], dbn6[:, :]))

            for b in range(AHEAD):
                clear()
                extract(b, b)
            dve.wait_ge(nodes_loaded, 16)
            dve.memset(nodes[:, :, H + F:H + F + 1], 1.0)
            dense_rows(0)

            def turn(b, i, tail):
                clear()
                scores(b, i)
                products(b, i)
                if not tail or b + AHEAD < NB:
                    extract(b + AHEAD, (i + AHEAD) % RING)
                if i == RING - 1:
                    finish(b - (RING - 1))
                if isinstance(b, int) and b == RING - 1:
                    dve.tensor_copy(x_sb[0:R, 0, :], dy[:, :])
                    dve.tensor_copy(stats[0:R, 0, :], dmv[:, :])
                    dve.memset(over[0:R, 0:1], 0.0).then_inc(d_out, 1)

            every_block(dve, turn)
            dve.wait_ge(d_out, 1)
            dve.sem_inc(over_ready, 1)
            dve.tensor_scalar(var[:, :], stats[:, :, 1], EPS, None, ALU.add).then_inc(var_ready, 1)
            dve.wait_ge(std_ready, 1)
            step(dve.reciprocal(rstd[:, :], std[:, :]))
            for c in range(STORES):
                o = slice(c * CH, (c + 1) * CH)
                full = [P, CH, F]
                step(dve.tensor_tensor(x_sb[:, o, :], x_sb[:, o, :], stats[:, o, 0].unsqueeze(2).to_broadcast(full), ALU.subtract))
                dve.tensor_tensor(x_sb[:, o, :], x_sb[:, o, :], rstd[:, o].unsqueeze(2).to_broadcast(full), ALU.mult).then_inc(out_ready, 1)

            dve.wait_ge(groups_summed, 1)
            clear()
            step(dve.memset(gzero, 0.0))
            step(dve.tensor_scalar(gflag_f.rearrange("o (b q) -> o b q", q=GPB), flag_ps.rearrange("o (q b) -> o b q", b=NB),
                                   0.0, None, ALU.is_gt))
            step(dve.tensor_tensor_scan(gcount, gflag_f, gzero, 1.0, ALU.add, ALU.add))
            step(dve.tensor_tensor(gturn[:, :], gcount, gflag_f, ALU.subtract))
            step(dve.tensor_copy(gflag[:, :], gflag_f))
            step(dve.tensor_reduce(bflag_f[:, :], gflag_f.rearrange("o (b q) -> o b q", q=GPB), AX.X, ALU.max))
            step(dve.tensor_copy(bflag[:, :], bflag_f[:, :]))
            dve.tensor_reduce(aflag[:, :], bflag_f[:, :], AX.X, ALU.max).then_inc(flags_ready, 1)

            def dense_group(g, n):
                dense_rows(n)
                dve.tensor_scalar(dvar[:, :], dmv[:, 1:2], EPS, None, ALU.add).then_inc(d_var, 1)
                wait_apart(dve, d_std, n)
                step(dve.reciprocal(drstd[:, :], dstd[:, :]))
                dve.tensor_scalar(dy[:, :], dy[:, :], dmv[:, 0:1], drstd[:, :], ALU.subtract, ALU.mult).then_inc(d_out, 1)

            flagged_groups(dve, dense_group)

_INS = ["x", "adj", "L0_gnn_W", "L0_gnn_att_self", "L0_gnn_att_neigh", "L0_gnn_bias"]


def kernel(**inputs):
    import numpy as _np
    import concourse.bacc as _bacc
    from concourse import mybir as _mybir
    from concourse.bass_utils import run_bass_kernel_spmd as _run

    nc = _bacc.Bacc("TRN2", target_bir_lowering=False, num_devices=1)
    arrays, args = {}, []
    for name in _INS:
        a = _np.ascontiguousarray(inputs[name])
        arrays[f"in_{name}_dram"] = a
        args.append(nc.dram_tensor(f"in_{name}_dram", a.shape, _mybir.dt.from_np(a.dtype), kind="ExternalInput").ap())
    out = nc.dram_tensor("out_dram", inputs["x"].shape, _mybir.dt.float32, kind="ExternalOutput").ap()
    gat_resnorm(nc, *args, out)
    r = _run(nc, [arrays], core_ids=[0])
    return r.results[0]["out_dram"]
```

```python
import concourse.bass as bass
from concourse import mybir
from contextlib import ExitStack


def gat_resnorm(nc, x, adj, w, att_self, att_neigh, bias, out):
    fp32, bf16 = mybir.dt.float32, mybir.dt.bfloat16
    i32, u32 = mybir.dt.int32, mybir.dt.uint32
    ALU, ACT, AX = mybir.AluOpType, mybir.ActivationFunctionType, mybir.AxisListType

    N, F = x.shape
    H, D = att_self.shape
    P = 128
    NB = N // P
    BITS = 16
    GC = N // BITS
    QUARTERS = 4
    SC = H + F
    TC = SC + 1
    PC = SC + H
    GB = 4
    NG = NB // GB
    SLOPE = 0.2
    EPS = 1e-5
    FAR = -1e30
    R = 16
    J = N // P
    GPB = P // R
    NGR = N // R
    RING = 4
    HEAD = 2
    REST = RING - 1
    NT = NB // RING
    NH = NT
    PARTS = 4
    UNROLLED = 4
    SLOTS = 16
    MORE_SLOTS = [56, 32] + [24] * (NH - 2)
    PAST = 1e5
    AHEAD = 4
    PARTS_X = [slice(0, NH)] + [slice(NH + c * REST * NT // 4, NH + (c + 1) * REST * NT // 4) for c in range(4)]
    PARTS_OUT = [slice(NH, NH + REST * NT // 2), slice(NH + REST * NT // 2, NB - REST), slice(0, NH - 1),
                 slice(NB - REST, NB), slice(NH - 1, NH)]
    COMPLETE = 3
    BY_POOL = 2
    PB = 512
    S_MAX = max(MORE_SLOTS)

    def block_at(t, i):
        if i == HEAD:
            return t
        return NH + REST * t + rank(i)

    def rank(i):
        return REST if i == HEAD else i - (i > HEAD)

    def plan(t, i):
        if i != HEAD:
            return SLOTS, 6
        return MORE_SLOTS[block_at(t, i) if isinstance(t, int) else UNROLLED], 8

    def later(t, i, d):
        return t + (i + d) // RING, (i + d) % RING

    ctx = ExitStack()
    with ctx:
        def sb(name, shape, dt):
            return ctx.enter_context(nc.sbuf_tensor(name, shape, dt))

        def pb(name, shape, dt):
            return ctx.enter_context(nc.psum_tensor(name, shape, dt))

        def sem(name):
            return ctx.enter_context(nc.semaphore(name))

        table = nc.dram_tensor("node_table", [N + 1, TC], fp32)
        own_table = nc.dram_tensor("own_table", [N, H], fp32)

        adj_sb = sb("adj_sb", [P, 2 * QUARTERS, N // QUARTERS], fp32)
        x_sb = sb("x_sb", [P, NB, F], fp32)
        own = sb("own", [P, NB, H], fp32)
        w_sb = sb("w_sb", [F, F], fp32)
        an_sb = sb("an_sb", [F, F], fp32)
        as_sb = sb("as_sb", [F, F], fp32)
        wtmp = sb("wtmp", [F, F], fp32)
        wa = sb("wa", [F, PC], fp32)
        bias_sb = sb("bias_sb", [P, F], fp32)
        ident = sb("ident", [P, P], fp32)
        weights = sb("weights", [P, BITS, P], bf16)
        ones = sb("ones", [P, 1], fp32)
        one_i = sb("one_i", [P, BITS], i32)
        bit_i = sb("bit_i", [P, BITS], i32)
        pow_i = sb("pow_i", [P, BITS], i32)
        pow_f = sb("pow_f", [P, BITS], fp32)
        off_i = sb("off_i", [P, BITS], i32)
        off_f = sb("off_f", [P, BITS], fp32)
        work = sb("work", [P, GC], fp32)
        val = sb("val", [P, S_MAX], fp32)
        col = sb("col", [P, S_MAX], u32)
        val_i = sb("val_i", [P, S_MAX], i32)
        hit = sb("hit", [P, S_MAX, BITS], i32)
        keys = sb("keys", [P, S_MAX, BITS], fp32)
        key = [sb(f"key{i}", [P, S_MAX], fp32) for i in range(RING)]
        absent = [sb(f"absent{i}", [P, S_MAX], fp32) for i in range(RING)]
        idx = [sb(f"idx{i}", [P, S_MAX], u32) for i in range(RING)]
        sign = sb("sign", [1, S_MAX], fp32)
        count_f = sb("count_f", [1, RING], fp32)
        count_i = sb("count_i", [1, RING], i32)
        over = sb("over", [P, NB], fp32)
        near = [sb(f"near{i}", [P, n, TC], fp32) for i, n in enumerate([S_MAX if i == HEAD else SLOTS for i in range(RING)])]
        z = sb("z", [P, S_MAX, H], fp32)
        lz = sb("lz", [P, S_MAX, H], fp32)
        top = sb("top", [P, H], fp32)
        sums = sb("sums", [P, RING, SC], fp32)
        rden = sb("rden", [P, RING, H], fp32)
        att = sb("att", [P, RING, F], fp32)
        bn6 = sb("bn6", [P, RING, 6], fp32)
        mv = sb("mv", [P, RING, 2], fp32)
        stats = sb("stats", [P, NB, 2], fp32)
        var = sb("var", [P, NB], fp32)
        std = sb("std", [P, NB], fp32)
        rstd = sb("rstd", [P, NB], fp32)
        nodes = sb("nodes", [P, J, TC], fp32)
        score = sb("score", [P, J, R * H], fp32)
        spare = score[:, :, :].rearrange("p j k -> p (j k)")
        n_xt, n_ft = 2 * GB * P, NB * TC
        xt_sb = spare[0:F, 0:n_xt].rearrange("p (i c) -> p i c", i=2)
        feat_sb = spare[:, n_xt:n_xt + n_ft].rearrange("p (b c) -> p b c", c=TC)
        arow = sb("arow", [P, R, J], fp32)
        own_r = sb("own_r", [P, R, H], fp32)
        x_r = sb("x_r", [R, F], fp32)
        dmax = sb("dmax", [P, R * H], fp32)
        dcol = sb("dcol", [P, 1], fp32)
        dtile = sb("dtile", [P, R * H], fp32)
        drden = sb("drden", [P, 1], fp32)
        dnum = sb("dnum", [P, F], fp32)
        datt = sb("datt", [R, F], fp32)
        dy = sb("dy", [R, F], fp32)
        dbn6 = sb("dbn6", [R, 6], fp32)
        dmv = sb("dmv", [R, 2], fp32)
        dvar = sb("dvar", [R, 1], fp32)
        dstd = sb("dstd", [R, 1], fp32)
        drstd = sb("drstd", [R, 1], fp32)
        head8 = sb("head8", [P, H], fp32)
        head_mask = sb("head_mask", [P, F], fp32)
        row_sel = sb("row_sel", [P, R], fp32)
        group_sel = sb("group_sel", [P, GPB], fp32)
        gflag_f = hit[0:1, 0:NGR // BITS, :].rearrange("o s k -> o (s k)").bitcast(fp32)
        gcount = keys[0:1, 0:NGR // BITS, :].rearrange("o s k -> o (s k)")
        gzero = work[0:1, 0:NGR]
        gany = lz[0:1, 0:NT * GPB // H, :].rearrange("o s h -> o (s h)").rearrange("o (t q) -> o t q", q=GPB)
        gflag = sb("gflag", [1, NGR], i32)
        gturn = sb("gturn", [1, NGR], i32)
        bflag = sb("bflag", [1, NB], i32)
        bflag_f = sb("bflag_f", [1, NB], fp32)
        aflag = sb("aflag", [1, 1], i32)

        codes = [pb(f"codes{i}", [P, GC], fp32) for i in range(RING)]
        xt_ps = [pb(f"xt_ps{i}", [P, GB * P], fp32) for i in range(2)]
        ft_ps = [pb(f"ft_ps{i}", [P, PB], fp32) for i in range(2)]
        count_ps = [ft_ps[1][0:1, P + i * S_MAX:P + (i + 1) * S_MAX] for i in range(RING)]
        max_ps = xt_ps[0][:, 0:R * H]
        maxrow_ps = xt_ps[0][:, R * H:2 * R * H]
        dsum_ps = ft_ps[0][:, 0:F + 1]
        drow_ps = xt_ps[0][0:R, 2 * R * H:2 * R * H + F]
        flag_ps = codes[0][0:1, 0:NGR]

        params_loaded = sem("params_loaded")
        bias_loaded = sem("bias_loaded")
        x_loaded = [sem(f"x_loaded{i}") for i in range(len(PARTS_X))]
        adj_loaded = [sem(f"adj_loaded{i}") for i in range(2 * QUARTERS)]
        ident_ready = sem("ident_ready")
        iotas_ready = sem("iotas_ready")
        near_zeroed = sem("near_zeroed")
        ones_ready = sem("ones_ready")
        dve_done = sem("dve_done")
        weights_ready = sem("weights_ready")
        wa_ready = sem("wa_ready")
        x_transposed = sem("x_transposed")
        xt_copied = sem("xt_copied")
        feats_ready = sem("feats_ready")
        feats_copied = sem("feats_copied")
        table_written = sem("table_written")
        own_written = sem("own_written")
        nodes_loaded = sem("nodes_loaded")
        quarters_packed = sem("quarters_packed")
        codes_read = sem("codes_read")
        keys_ready = sem("keys_ready")
        keys_counted = sem("keys_counted")
        signs_summed = sem("signs_summed")
        count_ready = sem("count_ready")
        idx_ready = sem("idx_ready")
        gathered = [sem(f"gathered{i}") for i in range(RING)]
        rows_ready = sem("rows_ready")
        scores_ready = sem("scores_ready")
        probs_ready = sem("probs_ready")
        slots_summed = sem("slots_summed")
        var_ready = sem("var_ready")
        std_ready = sem("std_ready")
        rstd_ready = sem("rstd_ready")
        centred = sem("centred")
        out_ready = [sem(f"out_ready{i}") for i in range(len(PARTS_OUT))]
        stored = sem("stored")
        over_ready = sem("over_ready")
        groups_summed = sem("groups_summed")
        flags_ready = sem("flags_ready")
        turns_ready = sem("turns_ready")
        d_loaded = sem("d_loaded")
        d_max = sem("d_max")
        d_max_t = sem("d_max_t")
        d_max_col = sem("d_max_col")
        d_max_row = sem("d_max_row")
        d_scores = sem("d_scores")
        d_probs = sem("d_probs")
        d_sums = sem("d_sums")
        d_scaled = sem("d_scaled")
        d_rows = sem("d_rows")
        d_var = sem("d_var")
        d_std = sem("d_std")
        d_out = sem("d_out")
        d_stored = sem("d_stored")
        waits_passed = sem("waits_passed")

        def of_dram(a, blocks):
            rows = a[blocks.start * P:blocks.stop * P, :]
            if blocks.start < NH:
                return rows.rearrange("(b p) c -> p b c", p=P)
            return rows.rearrange("(t p j) c -> p t (j c)", p=P, j=REST)

        def of_sbuf(a, blocks):
            return a[:, blocks, :] if blocks.start < NH else a[:, blocks, :].rearrange("p (t j) c -> p t (j c)", j=REST)

        adj_heads = adj[0:NH * P, :].rearrange("(b p) (h c) -> p b h c", p=P, h=QUARTERS)
        adj_rest = adj[NH * P:N, :].rearrange("(t p j) (h c) -> p t j h c", p=P, j=REST, h=QUARTERS)
        table_r = table[1:N + 1, :]
        adj_bf = [adj_sb[:, q, :].bitcast(bf16).rearrange("p (c two) -> p c two", two=2) for q in range(2 * QUARTERS)]

        def wait_apart(eng, signal, value):
            eng.wait_ge(signal, value)
            eng.sem_inc(waits_passed, 1)

        def every_block(eng, turn):
            for n in range(RING * UNROLLED):
                turn(n // RING, n % RING)
            with eng.Fori(UNROLLED, NT - 1) as t:
                for i in range(RING):
                    turn(t, i)
            for i in range(RING):
                turn(NT - 1, i)

        def flagged_groups(eng, body, before=None):
            eng.wait_ge(flags_ready, 1)
            any_at_all = eng.value_load(aflag[0:1, 0:1], min_val=0, max_val=1)
            with eng.If(any_at_all > 0):
                if before:
                    before()
                eng.wait_ge(turns_ready, 1)
                with eng.Fori(0, NB) as b:
                    any_group = eng.value_load(bflag[0:1, bass.ds(b, 1)], min_val=0, max_val=1)
                    with eng.If(any_group > 0):
                        with eng.Fori(0, GPB) as q:
                            g = b * GPB + q
                            this_group = eng.value_load(gflag[0:1, bass.ds(g, 1)], min_val=0, max_val=1)
                            with eng.If(this_group > 0):
                                turn = eng.value_load(gturn[0:1, bass.ds(g, 1)], min_val=1, max_val=NGR)
                                body(g, turn)

        block = ctx.enter_context(nc.Block())

        @block.sync
        def _(sp):
            def flat(a, n):
                return a.rearrange("h d -> (h d)").partition_broadcast(n)

            sp.dma_start(w_sb[:, :], w).then_inc(params_loaded, 16)
            sp.dma_start(an_sb[:, :], flat(att_neigh, F)).then_inc(params_loaded, 16)
            sp.dma_start(as_sb[:, :], flat(att_self, F)).then_inc(params_loaded, 16)
            for c, part in enumerate(PARTS_X):
                sp.dma_start(of_sbuf(x_sb, part), of_dram(x, part)).then_inc(x_loaded[c], 16)

            def load(t, i):
                n = RING * t + i
                for h in range(QUARTERS):
                    if not isinstance(n, int) or n >= 2:
                        sp.wait_ge(quarters_packed, QUARTERS * (n - 2) + h + 1)
                    q = QUARTERS * (i % 2) + h
                    rows = adj_heads[:, block_at(t, i), h, :] if i == HEAD else adj_rest[:, t, rank(i), h, :]
                    sp.dma_start(adj_sb[:, q, :], rows).then_inc(adj_loaded[q], 16)

            sp.dma_start(bias_sb[:, :], flat(bias, P)).then_inc(bias_loaded, 16)
            for n in range(RING * UNROLLED):
                load(n // RING, n % RING)
            with sp.Fori(UNROLLED, NT) as t:
                for i in range(RING):
                    load(t, i)
            for c, part in enumerate(PARTS_OUT):
                sp.wait_ge(out_ready[c], 1)
                sp.dma_start(of_dram(out, part), of_sbuf(x_sb, part)).then_inc(stored, 16)
            sp.wait_ge(stored, 16 * len(PARTS_OUT))

        @block.gpsimd
        def _(pool):
            pool.memset(ident[:, :], 0.0).then_inc(ident_ready, 1)
            pool.wait_ge(ident_ready, 1)
            pool.affine_select(out=ident[:, :], in_=ident[:, :], compare_op=ALU.not_equal, fill=1.0,
                               base=0, pattern=[[-1, P]], channel_multiplier=1).then_inc(ident_ready, 1)
            pool.iota(bit_i[:, :], [[1, BITS]], base=0, channel_multiplier=0).then_inc(iotas_ready, 1)
            pool.iota(off_i[:, :], [[GC, BITS]], base=1, channel_multiplier=0).then_inc(iotas_ready, 1)
            pool.memset(ones[:, :], 1.0).then_inc(ones_ready, 1)
            for i in range(RING):
                pool.memset(near[i][:, :, :], 0.0).then_inc(near_zeroed, 1)

            pool.wait_ge(table_written, 16 * (len(PARTS_X) + 1))
            pool.wait_ge(near_zeroed, RING)

            def gather(t, i):
                S, first = plan(t, i)
                n = RING * t + i
                wait_apart(pool, idx_ready, n + 1)
                wait_apart(pool, count_ready, n + 1)
                more = pool.value_load(count_i[0:1, i:i + 1], min_val=0, max_val=S_MAX)
                if not isinstance(n, int) or n >= RING:
                    wait_apart(pool, slots_summed, n - 3)

                def slot(k):
                    pool.indirect_dma_start(
                        out=near[i][:, k, :], out_offset=None, in_=table[:, :],
                        in_offset=bass.IndirectOffsetOnAxis(ap=idx[i][:, k:k + 1], axis=0),
                        bounds_check=N, oob_is_err=False).then_inc(gathered[i], 16)

                def slots_behind(k):
                    if k < S:
                        with pool.If(more > k - first):
                            slot(k)
                            slots_behind(k + 1)

                for k in range(first):
                    slot(k)
                slots_behind(first)

            every_block(pool, gather)
            pool.wait_ge(rstd_ready, 1)
            for c, part in enumerate(PARTS_OUT[:BY_POOL]):
                full = [P, part.stop - part.start, F]
                pool.tensor_tensor(x_sb[:, part, :], x_sb[:, part, :], stats[:, part, 0].unsqueeze(2).to_broadcast(full),
                                   ALU.subtract).then_inc(centred, 1)
                pool.wait_ge(centred, c + 1)
                pool.tensor_tensor(x_sb[:, part, :], x_sb[:, part, :], rstd[:, part].unsqueeze(2).to_broadcast(full),
                                   ALU.mult).then_inc(out_ready[c], 1)

        @block.scalar
        def _(act):
            def store_part(c):
                part = PARTS_X[c]
                act.wait_ge(feats_copied, part.stop // GB)
                act.dma_start(of_dram(table_r, part), of_sbuf(feat_sb, part)).then_inc(table_written, 16)
                if c == 0:
                    act.dma_start(table[0:1, :], feat_sb[0:1, 0, :]).then_inc(table_written, 16)

            for g in range(NG):
                act.wait_ge(x_transposed, g + 1)
                if g >= 2:
                    act.wait_ge(feats_ready, g - 1)
                act.activation(xt_sb[:, g % 2, :], xt_ps[g % 2][0:F, :], ACT.Copy).then_inc(xt_copied, 1)
                for c, part in enumerate(PARTS_X):
                    if part.stop == (g - 1) * GB:
                        store_part(c)
            store_part(len(PARTS_X) - 1)

            def count_slots(t, i):
                n = RING * t + i
                S, first = plan(t, i)
                wait_apart(act, keys_counted, n + 1)
                act.activation(sign[:, first:S], count_ps[i][:, first:S], ACT.Sign, accum_out=count_f[:, i:i + 1]).then_inc(signs_summed, 1)
                wait_apart(act, signs_summed, n + 1)
                act.activation(count_i[:, i:i + 1], count_f[:, i:i + 1], ACT.Copy).then_inc(count_ready, 1)

            def dense_loads(g):
                rows = bass.ds(g * R, R)
                act.dma_start(arow[:, :, :], adj[rows, :].rearrange("r (p j) -> p r j", j=J)).then_inc(d_loaded, 16)
                act.dma_start(own_r[:, :, :], own_table[rows, :].partition_broadcast(P)).then_inc(d_loaded, 16)
                act.dma_start(x_r[:, :], x[rows, :]).then_inc(d_loaded, 16)

            for i in range(2):
                count_slots(0, i)

            for part in (slice(0, NH), slice(NH, NB)):
                act.dma_start(of_dram(own_table, part), of_sbuf(own, part)).then_inc(own_written, 16)
            act.wait_ge(table_written, 16 * (len(PARTS_X) + 1))
            act.dma_start(nodes[:, :, :], table_r.rearrange("(p j) c -> p j c", j=J)).then_inc(nodes_loaded, 16)
            act.wait_ge(own_written, 32)
            dense_loads(0)

            for i in range(2, AHEAD):
                count_slots(0, i)

            def dense_exps(n):
                wait_apart(act, d_scores, n + 1)
                act.activation(score[:, :, :], score[:, :, :], ACT.Exp).then_inc(d_probs, 1)

            def take_root(k):
                act.wait_ge(var_ready, k + 1)
                act.activation(std[:, :], var[:, :], ACT.Sqrt).then_inc(std_ready, 1)

            issued = [act.alloc_register(f"issued{i}") for i in range(RING)]
            more_16 = act.alloc_register("more_16")
            for i in range(RING):
                act.reg_mov(issued[i], 0)

            def turn(t, i):
                n = RING * t + i
                S, first = plan(t, i)
                more = act.value_load(count_i[0:1, i:i + 1], min_val=0, max_val=S_MAX)
                act.reg_mul(more_16, more, 16)
                act.reg_add(issued[i], issued[i], more_16)
                act.reg_add(issued[i], issued[i], 16 * first)
                wait_apart(act, gathered[i], act.snap(issued[i]))
                act.sem_inc(rows_ready, 1)
                wait_apart(act, scores_ready, n + 1)
                act.activation(near[i][:, 0:S, 0:H], lz[:, 0:S, :], ACT.Exp).then_inc(probs_ready, 1)
                if not isinstance(n, int) or n + AHEAD < NB:
                    count_slots(*later(t, i, AHEAD))
                if isinstance(n, int) and n == 5:
                    dense_exps(0)
                if isinstance(n, int) and n == NB - 2:
                    take_root(0)

            every_block(act, turn)
            take_root(1)
            act.wait_ge(stored, 16 * len(PARTS_OUT))

            def dense_group(g, n):
                wait_apart(act, d_out, n)
                dense_loads(g)
                dense_exps(n)
                wait_apart(act, d_var, n)
                act.activation(dstd[:, :], dvar[:, :], ACT.Sqrt).then_inc(d_std, 1)
                wait_apart(act, d_out, n + 1)
                act.dma_start(out[bass.ds(g * R, R), :], dy[:, :]).then_inc(d_stored, 16)
                wait_apart(act, d_stored, 16 * n)

            flagged_groups(act, dense_group)

        @block.tensor
        def _(pe):
            def transpose(g):
                for c, part in enumerate(PARTS_X):
                    if part.start == g * GB:
                        pe.wait_ge(x_loaded[c], 16)
                if g >= 2:
                    pe.wait_ge(xt_copied, g - 1)
                for j in range(GB):
                    last = pe.transpose(xt_ps[g % 2][0:F, j * P:(j + 1) * P], x_sb[:, g * GB + j, :], ident[:, :])
                last.then_inc(x_transposed, 1)

            def project(g):
                pe.wait_ge(xt_copied, g + 1)
                if g >= 2:
                    pe.wait_ge(feats_copied, g - 1)
                for j in range(GB):
                    last = pe.matmul(ft_ps[g % 2][:, j * PC:(j + 1) * PC], xt_sb[:, g % 2, j * P:(j + 1) * P], wa[:, :],
                                     start=True, stop=True)
                last.then_inc(feats_ready, 1)

            def pack(t, i):
                n = RING * t + i
                if not isinstance(n, int) or n >= RING:
                    wait_apart(pe, codes_read, n - 3)
                for h in range(QUARTERS):
                    q = QUARTERS * (i % 2) + h
                    wait_apart(pe, adj_loaded[q], 16 * (2 * t + i // 2 + 1))
                    for k in range(BITS // QUARTERS):
                        kk = h * BITS // QUARTERS + k
                        last = pe.matmul(codes[i][:, :], weights[:, kk, :], adj_bf[q][:, k * GC:(k + 1) * GC, 1],
                                         start=(kk == 0), stop=(kk == BITS - 1))
                    last.then_inc(quarters_packed, 1)

            def count_keys(t, i):
                S = plan(t, i)[0]
                n = RING * t + i
                if not isinstance(n, int) or n > 0:
                    wait_apart(pe, signs_summed, n)
                wait_apart(pe, keys_ready, n + 1)
                pe.matmul(count_ps[i][:, 0:S], ones[:, :], key[i][:, 0:S], start=True, stop=True).then_inc(keys_counted, 1)

            pe.wait_ge(ident_ready, 2)
            transpose(0)
            pe.wait_ge(wa_ready, 1)
            for g in range(NG):
                if g + 1 < NG:
                    transpose(g + 1)
                project(g)
                if g == NG * 5 // 8:
                    pe.wait_ge(weights_ready, 1)
                    pack(0, 0)
            pe.wait_ge(feats_copied, NG)
            pe.wait_ge(ones_ready, 1)

            def dense_max(n):
                wait_apart(pe, d_max, n + 1)
                pe.transpose(max_ps, dmax[:, :], ident[:, :]).then_inc(d_max_t, 1)

            def dense_max_row(n):
                wait_apart(pe, d_max_col, n + 1)
                pe.transpose(maxrow_ps, dtile[:, :], ident[:, :]).then_inc(d_max_row, 1)

            def dense_sums(n, part):
                if part == 0:
                    wait_apart(pe, d_probs, n + 1)
                for j in range(part * J // PARTS, (part + 1) * J // PARTS):
                    last = pe.matmul(dsum_ps, score[:, j, :], nodes[:, j, H:TC],
                                     start=(j == 0), stop=(j == J - 1))
                if part == PARTS - 1:
                    last.then_inc(d_sums, 1)

            def dense_heads(n):
                wait_apart(pe, d_scaled, n + 1)
                pe.matmul(drow_ps, row_sel[:, :], dnum[:, :], start=True, stop=True).then_inc(d_rows, 1)

            def dense_group(g, n):
                dense_max(n)
                dense_max_row(n)
                for part in range(PARTS):
                    dense_sums(n, part)
                dense_heads(n)

            def turn(t, i):
                n = RING * t + i
                if not isinstance(n, int) or n > 0:
                    pack(t, i)
                    count_keys(*later(t, i, -1))
                if isinstance(n, int):
                    if n == 7:
                        dense_max(0)
                    elif n == 8:
                        dense_max_row(0)
                    elif 11 <= n < 11 + PARTS:
                        dense_sums(0, n - 11)

            every_block(pe, turn)
            count_keys(*later(NT - 1, RING - 1, 0))
            dense_heads(0)
            pe.wait_ge(over_ready, 1)
            for q in range(GPB):
                last = pe.matmul(flag_ps[:, q * NB:(q + 1) * NB], group_sel[:, q:q + 1], over[:, :], start=True, stop=True)
            last.then_inc(groups_summed, 1)
            flagged_groups(pe, dense_group)

        @block.vector
        def _(dve):
            chain = {"n": 0}

            def step(ins):
                chain["n"] += 1
                ins.then_inc(dve_done, 1)
                dve.wait_ge(dve_done, chain["n"])

            def mark(ins):
                chain["n"] += 1
                ins.then_inc(dve_done, 1)
                return chain["n"]

            def clear():
                dve.sem_clear(dve_done)
                chain["n"] = 0

            dve.wait_ge(params_loaded, 48)
            for a_sb, o in ((an_sb, 0), (as_sb, H + F)):
                step(dve.tensor_tensor(wtmp[:, :], w_sb[:, :], a_sb[:, :], ALU.mult))
                step(dve.tensor_reduce(wa[:, o:o + H], wtmp[:, :].rearrange("f (h d) -> f h d", d=D), AX.X, ALU.add))
            dve.tensor_copy(wa[:, H:H + F], w_sb[:, :]).then_inc(wa_ready, 1)
            dve.wait_ge(iotas_ready, 2)
            dve.wait_ge(ident_ready, 2)
            step(dve.memset(one_i[:, :], 1))
            step(dve.tensor_tensor(pow_i[:, :], one_i[:, :], bit_i[:, :], ALU.logical_shift_left))
            step(dve.tensor_copy(pow_f[:, :], pow_i[:, :]))
            dve.tensor_copy(off_f[:, :], off_i[:, :])
            dve.tensor_tensor(weights[:, :, :], ident[:, :].unsqueeze(1).to_broadcast([P, BITS, P]),
                              pow_f[:, :].unsqueeze(2).to_broadcast([P, BITS, P]), ALU.mult).then_inc(weights_ready, 1)
            step(dve.tensor_reduce(head8[:, :], ident[:, :].rearrange("p (r h) -> p h r", h=H), AX.X, ALU.add))
            dve.tensor_copy(head_mask[:, :].rearrange("p (h d) -> p h d", d=D), head8[:, :].unsqueeze(2).to_broadcast([P, H, D]))
            dve.tensor_reduce(row_sel[:, :], ident[:, :].rearrange("p (r h) -> p r h", h=H), AX.X, ALU.add)
            dve.tensor_reduce(group_sel[:, :], ident[:, :].rearrange("p (q r) -> p q r", r=R), AX.X, ALU.add)

            dve.memset(feat_sb[:, :, SC:TC], 1.0)
            for g in range(NG):
                dve.wait_ge(feats_ready, g + 1)
                fv = ft_ps[g % 2][:, 0:GB * PC].rearrange("p (j c) -> p j c", c=PC)
                o = slice(g * GB, (g + 1) * GB)
                dve.tensor_copy(own[:, o, :], fv[:, :, SC:PC])
                dve.tensor_copy(feat_sb[:, o, 0:SC], fv[:, :, 0:SC]).then_inc(feats_copied, 1)

            def views(t, i):
                S = plan(t, i)[0]
                g = near[i]
                zf, lf = (a[:, 0:S, :].rearrange("p s h -> p (s h)") for a in (z, lz))
                return S, [P, S, H], g, zf, lf

            def add_own(t, i):
                S, full, g, zf, lf = views(t, i)
                dve.wait_ge(rows_ready, RING * t + i + 1)
                return mark(dve.tensor_tensor(z[:, 0:S, :], g[:, 0:S, 0:H],
                                              own[:, bass.ds(block_at(t, i), 1), :].to_broadcast(full), ALU.add))

            def add_absent(t, i):
                S, full, g, zf, lf = views(t, i)
                return mark(dve.tensor_tensor(z[:, 0:S, :], z[:, 0:S, :],
                                              absent[i][:, 0:S].unsqueeze(2).to_broadcast(full), ALU.add))

            def leaky(t, i):
                S, full, g, zf, lf = views(t, i)
                return mark(dve.scalar_tensor_tensor(lf, zf, SLOPE, zf, ALU.mult, ALU.max))

            def find_top(t, i):
                S, full, g, zf, lf = views(t, i)
                return mark(dve.tensor_reduce(top[:, :], lz[:, 0:S, :].rearrange("p s h -> p h s"), AX.X, ALU.max))

            def less_top(t, i):
                S, full, g, zf, lf = views(t, i)
                dve.tensor_tensor(lz[:, 0:S, :], lz[:, 0:S, :], top[:, :].unsqueeze(1).to_broadcast(full),
                                  ALU.subtract).then_inc(scores_ready, 1)

            def weigh(t, i):
                S, full, g, zf, lf = views(t, i)
                feat = g[:, 0:S, H:H + F].rearrange("p s (h d) -> p s h d", d=D)
                dve.wait_ge(probs_ready, RING * t + i + 1)
                return mark(dve.tensor_tensor(feat, feat, g[:, 0:S, 0:H].unsqueeze(3).to_broadcast([P, S, H, D]), ALU.mult))

            def sum_slots(t, i):
                S, full, g, zf, lf = views(t, i)
                dve.tensor_reduce(sums[:, rank(i), :], g[:, 0:S, 0:SC].rearrange("p s c -> p c s"), AX.X, ALU.add).then_inc(slots_summed, 1)

            def attend(t, i):
                for score_step in (add_own, add_absent, leaky, find_top):
                    dve.wait_ge(dve_done, score_step(t, i))
                less_top(t, i)
                dve.wait_ge(dve_done, weigh(t, i))
                sum_slots(t, i)

            def extract(t, i, beside=None):
                n = RING * t + i
                S = plan(t, i)[0]
                rounds = S // 8
                wait_apart(dve, quarters_packed, QUARTERS * (n + 1))
                src = codes[i][:, :]
                for r in range(rounds):
                    o = slice(8 * r, 8 * r + 8)
                    step(dve.max(val[:, o], src))
                    if r == 0:
                        replaced = mark(dve.match_replace(work[:, :], val[:, o], src, 0.0))
                        dve.max_index(col[:, o], val[:, o], src).then_inc(codes_read, 1)
                        src = work[:, :]
                        dve.wait_ge(dve_done, replaced)
                    elif r < rounds - 1:
                        dve.max_index(col[:, o], val[:, o], src)
                        step(dve.match_replace(work[:, :], val[:, o], src, 0.0))
                    else:
                        values = mark(dve.tensor_copy(val_i[:, 0:S], val[:, 0:S]))
                        columns = mark(dve.max_index(col[:, o], val[:, o], src))
                if beside:
                    own_added = add_own(*beside)
                full = [P, S, BITS]
                kv, hv = (a[:, 0:S, :].rearrange("p s k -> p (s k)") for a in (keys, hit))
                wait_apart(dve, codes_read, n + 1)
                dve.wait_ge(dve_done, values)
                bits = mark(dve.tensor_tensor(hit[:, 0:S, :], val_i[:, 0:S].unsqueeze(2).to_broadcast(full),
                                              pow_i[:, :].unsqueeze(1).to_broadcast(full), ALU.bitwise_and))
                if beside:
                    dve.wait_ge(dve_done, own_added)
                    absent_added = add_absent(*beside)
                dve.wait_ge(dve_done, columns)
                added = mark(dve.tensor_tensor(keys[:, 0:S, :], col[:, 0:S].unsqueeze(2).to_broadcast(full),
                                               off_f[:, :].unsqueeze(1).to_broadcast(full), ALU.add))
                if beside:
                    dve.wait_ge(dve_done, absent_added)
                    sloped = leaky(*beside)
                dve.wait_ge(dve_done, max(bits, added))
                masked = mark(dve.scalar_tensor_tensor(kv, hv, 0.0, kv, ALU.is_gt, ALU.mult))
                if beside:
                    dve.wait_ge(dve_done, sloped)
                    top_found = find_top(*beside)
                dve.wait_ge(dve_done, masked)
                for r in range(rounds):
                    o = slice(8 * r, 8 * r + 8)
                    ins = dve.max(key[i][:, o], kv)
                    if r < rounds - 1:
                        found = mark(ins)
                        if beside and r == 0:
                            dve.wait_ge(dve_done, top_found)
                            less_top(*beside)
                        dve.wait_ge(dve_done, found)
                        step(dve.match_replace(kv, key[i][:, o], kv, 0.0))
                ins.then_inc(keys_ready, 1)
                if beside:
                    weighted = weigh(*beside)
                wait_apart(dve, keys_ready, n + 1)
                marked = mark(dve.tensor_scalar(absent[i][:, 0:S], key[i][:, 0:S], 0.0, FAR, ALU.is_equal, ALU.mult))
                if beside:
                    dve.wait_ge(dve_done, weighted)
                    sum_slots(*beside)
                dve.wait_ge(dve_done, marked)
                dve.scalar_tensor_tensor(idx[i][:, 0:S], absent[i][:, 0:S], PAST / FAR, key[i][:, 0:S],
                                         ALU.mult, ALU.add).then_inc(idx_ready, 1)
                dve.scalar_tensor_tensor(over[:, bass.ds(block_at(t, i), 1)], absent[i][:, 0:1], -1.0, key[i][:, S - 1:S], ALU.mult, ALU.max)

            def finish(t):
                wait_apart(dve, slots_summed, RING * t + RING)
                step(dve.reciprocal(rden[:, :, :], sums[:, :, 0:H]))
                step(dve.tensor_tensor(att[:, :, :].rearrange("p i (h d) -> p i h d", d=D),
                                       sums[:, :, H:H + F].rearrange("p i (h d) -> p i h d", d=D),
                                       rden[:, :, :].unsqueeze(3).to_broadcast([P, RING, H, D]), ALU.mult))
                step(dve.tensor_tensor(att[:, :, :], att[:, :, :], bias_sb[:, :].unsqueeze(1).to_broadcast([P, RING, F]), ALU.add))
                parts = ((slice(0, REST), bass.ds(NH + REST * t, REST)), (slice(REST, RING), bass.ds(block_at(t, HEAD), 1)))
                for o, blocks in parts:
                    af = att[:, o, :].rearrange("p i f -> p (i f)")
                    xf = x_sb[:, blocks, :].rearrange("p i f -> p (i f)")
                    ins = dve.scalar_tensor_tensor(xf, af, 0.0, xf, ALU.max, ALU.add)
                step(ins)
                for i in range(RING):
                    ins = dve.bn_stats(bn6[:, rank(i), :], x_sb[:, bass.ds(block_at(t, i), 1), :].rearrange("p i f -> p (i f)"))
                step(ins)
                for i in range(RING):
                    ins = dve.bn_aggr(mv[:, i, :], bn6[:, i, :])
                step(ins)
                for o, blocks in parts:
                    ins = dve.tensor_copy(stats[:, blocks, :], mv[:, o, :])
                step(ins)

            full_d = [P, J, R, H]
            s4 = score[:, :, :].rearrange("p j (r h) -> p j r h", h=H)
            sf = score[:, :, :].rearrange("p j k -> p (j k)")

            def dense_add(n):
                wait_apart(dve, d_loaded, 48 * n + 48)
                if isinstance(n, int):
                    dve.wait_ge(nodes_loaded, 16)
                step(dve.tensor_tensor(s4, nodes[:, :, 0:H].unsqueeze(2).to_broadcast(full_d),
                                       own_r[:, :, :].unsqueeze(1).to_broadcast(full_d), ALU.add))

            def dense_leaky(n):
                step(dve.scalar_tensor_tensor(sf, sf, SLOPE, sf, ALU.mult, ALU.max))

            def dense_mask(n):
                step(dve.tensor_scalar(arow[:, :, :], arow[:, :, :], -1.0, 1e10, ALU.add, ALU.mult))
                step(dve.tensor_tensor(s4, s4, arow[:, :, :].rearrange("p r j -> p j r").unsqueeze(3).to_broadcast(full_d), ALU.add))

            def dense_max(n):
                dve.tensor_reduce(dmax[:, :], score[:, :, :].rearrange("p j k -> p k j"), AX.X, ALU.max).then_inc(d_max, 1)

            def dense_max_col(n):
                wait_apart(dve, d_max_t, n + 1)
                step(dve.tensor_reduce(dcol[:, :], max_ps, AX.X, ALU.max))
                dve.tensor_copy(dtile[:, :], dcol[:, :].to_broadcast([P, R * H])).then_inc(d_max_col, 1)

            def dense_less_max(n):
                wait_apart(dve, d_max_row, n + 1)
                dve.tensor_tensor(score[:, :, :], score[:, :, :], maxrow_ps.unsqueeze(1).to_broadcast([P, J, R * H]),
                                  ALU.subtract).then_inc(d_scores, 1)

            def dense_scale(n):
                wait_apart(dve, d_sums, n + 1)
                step(dve.reciprocal(drden[:, :], dsum_ps[:, F:F + 1]))
                dve.scalar_tensor_tensor(dnum[:, :], dsum_ps[:, 0:F], drden[:, :], head_mask[:, :], ALU.mult, ALU.mult).then_inc(d_scaled, 1)

            def dense_finish(n):
                wait_apart(dve, d_rows, n + 1)
                step(dve.tensor_tensor(datt[:, :], drow_ps, bias_sb[0:R, :], ALU.add))
                step(dve.scalar_tensor_tensor(dy[:, :], datt[:, :], 0.0, x_r[:, :], ALU.max, ALU.add))
                step(dve.bn_stats(dbn6[:, :], dy[:, :]))
                step(dve.bn_aggr(dmv[:, :], dbn6[:, :]))

            dense_steps = [dense_add, dense_leaky, dense_mask, dense_max, dense_max_col, dense_less_max,
                           dense_scale, dense_finish]
            dense_turns = {1: [dense_add, dense_leaky, dense_mask, dense_max], 3: [dense_max_col], 4: [dense_less_max],
                           NB - RING: [dense_scale]}

            def normalise(c, part):
                full = [P, part.stop - part.start, F]
                step(dve.tensor_tensor(x_sb[:, part, :], x_sb[:, part, :], stats[:, part, 0].unsqueeze(2).to_broadcast(full), ALU.subtract))
                dve.tensor_tensor(x_sb[:, part, :], x_sb[:, part, :], rstd[:, part].unsqueeze(2).to_broadcast(full), ALU.mult).then_inc(out_ready[c], 1)

            def invert_root(k):
                dve.wait_ge(std_ready, k + 1)
                for part in (PARTS_OUT[:COMPLETE], PARTS_OUT[COMPLETE:])[k]:
                    ins = dve.reciprocal(rstd[:, part], std[:, part])
                ins.then_inc(rstd_ready, 1)

            def add_eps():
                dve.tensor_scalar(var[:, :], stats[:, :, 1], EPS, None, ALU.add).then_inc(var_ready, 1)

            for i in range(AHEAD):
                clear()
                extract(0, i)
            dve.wait_ge(bias_loaded, 16)
            dve.memset(stats[:, :, :], 1.0)

            def turn(t, i):
                n = RING * t + i
                clear()
                if not isinstance(n, int) or n + AHEAD < NB:
                    extract(*later(t, i, AHEAD), beside=(t, i))
                else:
                    attend(t, i)
                if i == RING - 1:
                    finish(t)
                if isinstance(n, int):
                    for dense_step in dense_turns.get(n, []):
                        dense_step(0)
                if isinstance(n, int) and n == NB - 3:
                    dense_finish(0)
                    dve.tensor_copy(x_sb[0:R, 0, :], dy[:, :])
                    step(dve.tensor_copy(stats[0:R, 0, :], dmv[:, :]))
                    dve.memset(over[0:R, 0:1], 0.0).then_inc(d_out, 1)
                    add_eps()
                if isinstance(n, int) and n == NB - 2:
                    invert_root(0)

            every_block(dve, turn)
            clear()
            add_eps()
            invert_root(1)
            dve.wait_ge(rstd_ready, 2)
            for c in range(BY_POOL, len(PARTS_OUT)):
                normalise(c, PARTS_OUT[c])
            dve.wait_ge(d_out, 1)
            dve.sem_inc(over_ready, 1)

            dve.wait_ge(groups_summed, 1)
            clear()
            step(dve.tensor_reduce(bflag_f[:, 0:1], flag_ps, AX.X, ALU.max))
            dve.tensor_scalar(aflag[:, :], bflag_f[:, 0:1], 0.0, None, ALU.is_gt).then_inc(flags_ready, 1)

            def number_groups():
                clear()
                step(dve.memset(gzero, 0.0))
                step(dve.tensor_scalar(gflag_f[:, 0:NH * GPB].rearrange("o (b q) -> o b q", q=GPB),
                                       flag_ps.rearrange("o (q b) -> o b q", b=NB)[:, 0:NH, :], 0.0, None, ALU.is_gt))
                rest_f = flag_ps.rearrange("o (q b) -> o b q", b=NB)[:, NH:NB, :].rearrange("o (t j) q -> o t q j", j=REST)
                step(dve.tensor_reduce(gany, rest_f, AX.X, ALU.max))
                step(dve.tensor_scalar(gflag_f[:, NH * GPB:NGR].rearrange("o (x j) -> o x j", j=REST),
                                       gany.rearrange("o t q -> o (t q)").unsqueeze(2).to_broadcast([1, NT * GPB, REST]),
                                       0.0, None, ALU.is_gt))
                step(dve.tensor_tensor_scan(gcount, gflag_f, gzero, 1.0, ALU.add, ALU.add))
                step(dve.tensor_tensor(gturn[:, :], gcount, gflag_f, ALU.subtract))
                step(dve.tensor_copy(gflag[:, :], gflag_f))
                step(dve.tensor_reduce(bflag_f[:, :], gflag_f.rearrange("o (b q) -> o b q", q=GPB), AX.X, ALU.max))
                dve.tensor_copy(bflag[:, :], bflag_f[:, :]).then_inc(turns_ready, 1)

            def dense_group(g, n):
                clear()
                for dense_step in dense_steps:
                    dense_step(n)
                dve.tensor_scalar(dvar[:, :], dmv[:, 1:2], EPS, None, ALU.add).then_inc(d_var, 1)
                wait_apart(dve, d_std, n)
                step(dve.reciprocal(drstd[:, :], dstd[:, :]))
                dve.tensor_scalar(dy[:, :], dy[:, :], dmv[:, 0:1], drstd[:, :], ALU.subtract, ALU.mult).then_inc(d_out, 1)

            flagged_groups(dve, dense_group, number_groups)

_INS = ["x", "adj", "L0_gnn_W", "L0_gnn_att_self", "L0_gnn_att_neigh", "L0_gnn_bias"]


def kernel(**inputs):
    import numpy as _np
    import concourse.bacc as _bacc
    from concourse import mybir as _mybir
    from concourse.bass_utils import run_bass_kernel_spmd as _run

    nc = _bacc.Bacc("TRN2", target_bir_lowering=False, num_devices=1)
    arrays, args = {}, []
    for name in _INS:
        a = _np.ascontiguousarray(inputs[name])
        arrays[f"in_{name}_dram"] = a
        args.append(nc.dram_tensor(f"in_{name}_dram", a.shape, _mybir.dt.from_np(a.dtype), kind="ExternalInput").ap())
    out = nc.dram_tensor("out_dram", inputs["x"].shape, _mybir.dt.float32, kind="ExternalOutput").ap()
    gat_resnorm(nc, *args, out)
    r = _run(nc, [arrays], core_ids=[0])
    return r.results[0]["out_dram"]
```
